# Optimizing a Trainium2 kernel written in Bass

```python
import numpy as np
import jax
import jax.numpy as jnp

def _softmax(x, axis=-1):
    return jax.nn.softmax(x, axis=axis)

def _gelu(x):
    return jax.nn.gelu(x, approximate=True)

def _silu(x):
    return jax.nn.silu(x)

def _sigmoid(x):
    return jax.nn.sigmoid(x)

def _layernorm(x, axis=-1, eps=1e-05):
    m = jnp.mean(x, axis=axis, keepdims=True)
    v = jnp.var(x, axis=axis, keepdims=True)
    return (x - m) / jnp.sqrt(v + eps)

def _scatter_add(tgt, idx, src, axis=0):
    return tgt.at[idx].add(src)

def _segment_sum(src, seg, n):
    return jax.ops.segment_sum(src, seg, n)
kernel_name = 'mk_vit_tower_d1_tok_img768_r4_6791bc'

def setup_inputs(seed: int=0):
    np.random.seed(seed)
    _w = jnp.asarray

    def _rec_inputs():
        import jax
        import jax.numpy as jnp
        _rk = jax.random.key(seed)
        x = 7.57192e-06 + 1.00007 * jax.random.normal(jax.random.fold_in(_rk, 1), (16, 3, 112, 112), jnp.float32)
        return x
    x = _rec_inputs()

    def _L0_tok_setup():
        import jax, jax.numpy as jnp
        import numpy as np
        EPS = 1e-05

        def _layernorm(x, g, b):
            mu = jnp.mean(x, axis=-1, keepdims=True)
            var = jnp.mean(jnp.square(x - mu), axis=-1, keepdims=True)
            return (x - mu) * jax.lax.rsqrt(var + EPS) * g + b

        def _patchify(x, p):
            B, C, H, W = x.shape
            h, w = (H // p, W // p)
            x = x.reshape(B, C, h, p, w, p)
            x = x.transpose(0, 2, 4, 3, 5, 1)
            return x.reshape(B, h * w, p * p * C)
        key = jax.random.key(seed)
        ks = jax.random.split(key, 3)
        B, C, S, P, D = (64, 3, 224, 16, 192)
        patch_dim = C * P * P
        x = jax.random.normal(ks[0], (B, C, S, S), dtype=jnp.float32)
        ln1_g = jnp.ones((patch_dim,), jnp.float32)
        ln1_b = jnp.zeros((patch_dim,), jnp.float32)
        bound = 1.0 / np.sqrt(patch_dim)
        W = jax.random.uniform(ks[1], (D, patch_dim), jnp.float32, -bound, bound)
        b = jax.random.uniform(ks[2], (D,), jnp.float32, -bound, bound)
        ln2_g = jnp.ones((D,), jnp.float32)
        ln2_b = jnp.zeros((D,), jnp.float32)
        return {'x': x, 'ln1_g': ln1_g, 'ln1_b': ln1_b, 'W': W, 'b': b, 'ln2_g': ln2_g, 'ln2_b': ln2_b}
    _L0_tok_all = _L0_tok_setup()
    _L0_tok_in = {k: v for k, v in _L0_tok_all.items() if k in ('ln1_g', 'ln1_b', 'W', 'b', 'ln2_g', 'ln2_b')}
    del _L0_tok_all

    def _L0_attn_setup():
        import jax, jax.numpy as jnp
        import numpy as np
        B, S, D_MODEL, N_HEAD, D_HEAD, GROUPS = (2, 256, 192, 12, 64, 4)
        EPS = 1e-09
        SCALE = 1.0 / np.sqrt(D_HEAD).astype(np.float32)

        def grouped_proj(x, W, b=None):
            g = W.shape[0]
            b_, s_, d = x.shape
            y = jnp.einsum('bsgi,gio->bsgo', x.reshape(b_, s_, g, d // g), W).reshape(b_, s_, -1)
            return y if b is None else y + b

        def rel_shift_gather(pos_attn, context_len, shift):
            b, n, s, m = pos_attn.shape
            pos_attn = pos_attn.reshape(b, n, m, s)[:, :, shift:, :]
            pos_attn = pos_attn.reshape(b, n, s, m - shift)[..., :context_len]
            return pos_attn
        key = jax.random.key(seed)
        ks = jax.random.split(key, 16)
        dg = D_MODEL // GROUPS
        og = N_HEAD * D_HEAD // GROUPS
        std = 0.02
        return {'query': jax.random.normal(ks[0], (B, S, D_MODEL), jnp.float32), 'position_embeds': jax.random.normal(ks[1], (2 * S - 1, D_MODEL), jnp.float32), 'Wq': jax.random.normal(ks[2], (GROUPS, dg, og), jnp.float32) * std, 'Wk': jax.random.normal(ks[3], (GROUPS, dg, og), jnp.float32) * std, 'bk': jnp.zeros((N_HEAD * D_HEAD,), jnp.float32), 'Wv': jax.random.normal(ks[4], (GROUPS, dg, dg), jnp.float32) * std, 'bv': jnp.zeros((D_MODEL,), jnp.float32), 'r_kernel': jax.random.normal(ks[5], (D_MODEL, N_HEAD, D_HEAD), jnp.float32) * std, 'r_w_bias': jax.random.normal(ks[6], (N_HEAD, D_HEAD), jnp.float32) * std, 'r_r_bias': jax.random.normal(ks[7], (N_HEAD, D_HEAD), jnp.float32) * std, 'Wo': jax.random.normal(ks[8], (D_MODEL, D_MODEL), jnp.float32) * std, 'bo': jnp.zeros((D_MODEL,), jnp.float32), 'gamma': jnp.ones((D_MODEL,), jnp.float32), 'beta': jnp.zeros((D_MODEL,), jnp.float32)}
    _L0_attn_all = _L0_attn_setup()
    _L0_attn_in = {k: v for k, v in _L0_attn_all.items() if k in ('position_embeds', 'Wq', 'Wk', 'bk', 'Wv', 'bv', 'r_kernel', 'r_w_bias', 'r_r_bias', 'Wo', 'bo', 'gamma', 'beta')}
    del _L0_attn_all

    def _L0_ffn_setup():
        import jax, jax.numpy as jnp
        import numpy as np
        H = 12
        ALPHA = (1, 2, 3)
        DEPTH = 5
        BLOCK_DEPTH = 3
        TOTAL_DEPTH_M1 = 14 - 1
        SMALL_ACTIVE = BLOCK_DEPTH <= DEPTH <= TOTAL_DEPTH_M1 - BLOCK_DEPTH

        def _ln(x, g, b, eps=1e-05):
            m = jnp.mean(x, axis=-1, keepdims=True)
            v = jnp.mean((x - m) ** 2, axis=-1, keepdims=True)
            return (x - m) * jax.lax.rsqrt(v + eps) * g + b

        def _attn_branch(xp, w_qkv, w_proj, b_proj, keep_heads, keep_ch):
            B2, N, C = xp.shape
            hd = C // H
            scale = hd ** (-0.5)
            qkv = (xp @ w_qkv).reshape(B2, N, 3, H, hd).transpose(2, 0, 3, 1, 4)
            hmask = (jnp.arange(H) < keep_heads).astype(xp.dtype)[None, :, None, None]
            q, k, v = (qkv[0] * hmask, qkv[1] * hmask, qkv[2] * hmask)
            a = jax.nn.softmax(jnp.einsum('bhnd,bhmd->bhnm', q, k) * scale, axis=-1)
            o = jnp.einsum('bhnm,bhmd->bhnd', a, v).transpose(0, 2, 1, 3).reshape(B2, N, C)
            o = o @ w_proj + b_proj
            cmask = (jnp.arange(C) < keep_ch).astype(xp.dtype)
            return o * cmask

        def _mlp_branch(xp, w1, b1, w2, b2, keep_ch):
            C = xp.shape[-1]
            cmask = (jnp.arange(C) < keep_ch).astype(xp.dtype)
            h = jax.nn.gelu(xp * cmask @ w1 + b1, approximate=False)
            return (h @ w2 + b2) * cmask
        key = jax.random.key(seed)
        ks = jax.random.split(key, 8)
        B, N, C = (64, 257, 192)
        HID = 4 * C

        def w(k, shape):
            return jax.random.normal(k, shape, jnp.float32) * 0.02
        return {'x': jax.random.normal(ks[0], (B, N, C), jnp.float32), 'gumbel_weights': jax.random.uniform(ks[1], (3,), jnp.float32), 'n1l_g': jnp.ones((C,), jnp.float32), 'n1l_b': jnp.zeros((C,), jnp.float32), 'n1s_g': jnp.ones((C,), jnp.float32), 'n1s_b': jnp.zeros((C,), jnp.float32), 'w_qkv': w(ks[2], (C, 3 * C)), 'w_proj': w(ks[3], (C, C)), 'b_proj': jnp.zeros((C,), jnp.float32), 'n2l_g': jnp.ones((C,), jnp.float32), 'n2l_b': jnp.zeros((C,), jnp.float32), 'n2s_g': jnp.ones((C,), jnp.float32), 'n2s_b': jnp.zeros((C,), jnp.float32), 'w_fc1': w(ks[4], (C, HID)), 'b_fc1': jnp.zeros((HID,), jnp.float32), 'w_fc2': w(ks[5], (HID, C)), 'b_fc2': jnp.zeros((C,), jnp.float32)}
    _L0_ffn_all = _L0_ffn_setup()
    _L0_ffn_in = {k: v for k, v in _L0_ffn_all.items() if k in ('gumbel_weights', 'n1l_g', 'n1l_b', 'n1s_g', 'n1s_b', 'w_qkv', 'w_proj', 'b_proj', 'n2l_g', 'n2l_b', 'n2s_g', 'n2s_b', 'w_fc1', 'b_fc1', 'w_fc2', 'b_fc2')}
    del _L0_ffn_all
    return {'x': x, 'L0_tok_ln1_g': _L0_tok_in['ln1_g'], 'L0_tok_ln1_b': _L0_tok_in['ln1_b'], 'L0_tok_W': _L0_tok_in['W'], 'L0_tok_b': _L0_tok_in['b'], 'L0_tok_ln2_g': _L0_tok_in['ln2_g'], 'L0_tok_ln2_b': _L0_tok_in['ln2_b'], 'L0_attn_position_embeds': _L0_attn_in['position_embeds'], 'L0_attn_Wq': _L0_attn_in['Wq'], 'L0_attn_Wk': _L0_attn_in['Wk'], 'L0_attn_bk': _L0_attn_in['bk'], 'L0_attn_Wv': _L0_attn_in['Wv'], 'L0_attn_bv': _L0_attn_in['bv'], 'L0_attn_r_kernel': _L0_attn_in['r_kernel'], 'L0_attn_r_w_bias': _L0_attn_in['r_w_bias'], 'L0_attn_r_r_bias': _L0_attn_in['r_r_bias'], 'L0_attn_Wo': _L0_attn_in['Wo'], 'L0_attn_bo': _L0_attn_in['bo'], 'L0_attn_gamma': _L0_attn_in['gamma'], 'L0_attn_beta': _L0_attn_in['beta'], 'L0_ffn_gumbel_weights': _L0_ffn_in['gumbel_weights'], 'L0_ffn_n1l_g': _L0_ffn_in['n1l_g'], 'L0_ffn_n1l_b': _L0_ffn_in['n1l_b'], 'L0_ffn_n1s_g': _L0_ffn_in['n1s_g'], 'L0_ffn_n1s_b': _L0_ffn_in['n1s_b'], 'L0_ffn_w_qkv': _L0_ffn_in['w_qkv'], 'L0_ffn_w_proj': _L0_ffn_in['w_proj'], 'L0_ffn_b_proj': _L0_ffn_in['b_proj'], 'L0_ffn_n2l_g': _L0_ffn_in['n2l_g'], 'L0_ffn_n2l_b': _L0_ffn_in['n2l_b'], 'L0_ffn_n2s_g': _L0_ffn_in['n2s_g'], 'L0_ffn_n2s_b': _L0_ffn_in['n2s_b'], 'L0_ffn_w_fc1': _L0_ffn_in['w_fc1'], 'L0_ffn_b_fc1': _L0_ffn_in['b_fc1'], 'L0_ffn_w_fc2': _L0_ffn_in['w_fc2'], 'L0_ffn_b_fc2': _L0_ffn_in['b_fc2']}

def reference(x, L0_tok_ln1_g, L0_tok_ln1_b, L0_tok_W, L0_tok_b, L0_tok_ln2_g, L0_tok_ln2_b, L0_attn_position_embeds, L0_attn_Wq, L0_attn_Wk, L0_attn_bk, L0_attn_Wv, L0_attn_bv, L0_attn_r_kernel, L0_attn_r_w_bias, L0_attn_r_r_bias, L0_attn_Wo, L0_attn_bo, L0_attn_gamma, L0_attn_beta, L0_ffn_gumbel_weights, L0_ffn_n1l_g, L0_ffn_n1l_b, L0_ffn_n1s_g, L0_ffn_n1s_b, L0_ffn_w_qkv, L0_ffn_w_proj, L0_ffn_b_proj, L0_ffn_n2l_g, L0_ffn_n2l_b, L0_ffn_n2s_g, L0_ffn_n2s_b, L0_ffn_w_fc1, L0_ffn_b_fc1, L0_ffn_w_fc2, L0_ffn_b_fc2):
    import jax
    import jax.numpy as jnp

    def _L0_tok_ref(x, ln1_g, ln1_b, W, b, ln2_g, ln2_b):
        import jax, jax.numpy as jnp
        import numpy as np
        EPS = 1e-05

        def _layernorm(x, g, b):
            mu = jnp.mean(x, axis=-1, keepdims=True)
            var = jnp.mean(jnp.square(x - mu), axis=-1, keepdims=True)
            return (x - mu) * jax.lax.rsqrt(var + EPS) * g + b

        def _patchify(x, p):
            B, C, H, W = x.shape
            h, w = (H // p, W // p)
            x = x.reshape(B, C, h, p, w, p)
            x = x.transpose(0, 2, 4, 3, 5, 1)
            return x.reshape(B, h * w, p * p * C)
        p = 16
        patches = _patchify(x, p)
        h = _layernorm(patches, ln1_g, ln1_b)
        h = jnp.einsum('bnd,ed->bne', h, W) + b
        return _layernorm(h, ln2_g, ln2_b)

    def _L0_attn_ref(query, position_embeds, Wq, Wk, bk, Wv, bv, r_kernel, r_w_bias, r_r_bias, Wo, bo, gamma, beta):
        import jax, jax.numpy as jnp
        import numpy as np
        B, S, D_MODEL, N_HEAD, D_HEAD, GROUPS = (2, 256, 192, 12, 64, 4)
        EPS = 1e-09
        SCALE = 1.0 / np.sqrt(D_HEAD).astype(np.float32)

        def grouped_proj(x, W, b=None):
            g = W.shape[0]
            b_, s_, d = x.shape
            y = jnp.einsum('bsgi,gio->bsgo', x.reshape(b_, s_, g, d // g), W).reshape(b_, s_, -1)
            return y if b is None else y + b

        def rel_shift_gather(pos_attn, context_len, shift):
            b, n, s, m = pos_attn.shape
            pos_attn = pos_attn.reshape(b, n, m, s)[:, :, shift:, :]
            pos_attn = pos_attn.reshape(b, n, s, m - shift)[..., :context_len]
            return pos_attn
        b, s, _ = query.shape
        q = grouped_proj(query, Wq).reshape(b, s, N_HEAD, D_HEAD) * SCALE
        k = grouped_proj(query, Wk, bk).reshape(b, s, N_HEAD, D_HEAD)
        v = grouped_proj(query, Wv, bv).reshape(b, s, N_HEAD, D_MODEL // N_HEAD)
        content_score = jnp.einsum('bind,bjnd->bnij', q + r_w_bias * SCALE, k)
        r_head = jnp.einsum('td,dnh->tnh', position_embeds, r_kernel)
        pos_score = jnp.einsum('bind,tnd->bnit', q + r_r_bias * SCALE, r_head)
        pos_score = rel_shift_gather(pos_score, s, shift=1)
        attn_prob = jax.nn.softmax(content_score + pos_score, axis=-1)
        attn_vec = jnp.einsum('bnij,bjnd->bind', attn_prob, v).reshape(b, s, D_MODEL)
        attn_out = attn_vec @ Wo + bo
        h = query + attn_out
        mu = jnp.mean(h, axis=-1, keepdims=True)
        var = jnp.mean(jnp.square(h - mu), axis=-1, keepdims=True)
        return (h - mu) * jax.lax.rsqrt(var + EPS) * gamma + beta

    def _L0_ffn_ref(x, gumbel_weights, n1l_g, n1l_b, n1s_g, n1s_b, w_qkv, w_proj, b_proj, n2l_g, n2l_b, n2s_g, n2s_b, w_fc1, b_fc1, w_fc2, b_fc2):
        import jax, jax.numpy as jnp
        import numpy as np
        H = 12
        ALPHA = (1, 2, 3)
        DEPTH = 5
        BLOCK_DEPTH = 3
        TOTAL_DEPTH_M1 = 14 - 1
        SMALL_ACTIVE = BLOCK_DEPTH <= DEPTH <= TOTAL_DEPTH_M1 - BLOCK_DEPTH

        def _ln(x, g, b, eps=1e-05):
            m = jnp.mean(x, axis=-1, keepdims=True)
            v = jnp.mean((x - m) ** 2, axis=-1, keepdims=True)
            return (x - m) * jax.lax.rsqrt(v + eps) * g + b

        def _attn_branch(xp, w_qkv, w_proj, b_proj, keep_heads, keep_ch):
            B2, N, C = xp.shape
            hd = C // H
            scale = hd ** (-0.5)
            qkv = (xp @ w_qkv).reshape(B2, N, 3, H, hd).transpose(2, 0, 3, 1, 4)
            hmask = (jnp.arange(H) < keep_heads).astype(xp.dtype)[None, :, None, None]
            q, k, v = (qkv[0] * hmask, qkv[1] * hmask, qkv[2] * hmask)
            a = jax.nn.softmax(jnp.einsum('bhnd,bhmd->bhnm', q, k) * scale, axis=-1)
            o = jnp.einsum('bhnm,bhmd->bhnd', a, v).transpose(0, 2, 1, 3).reshape(B2, N, C)
            o = o @ w_proj + b_proj
            cmask = (jnp.arange(C) < keep_ch).astype(xp.dtype)
            return o * cmask

        def _mlp_branch(xp, w1, b1, w2, b2, keep_ch):
            C = xp.shape[-1]
            cmask = (jnp.arange(C) < keep_ch).astype(xp.dtype)
            h = jax.nn.gelu(xp * cmask @ w1 + b1, approximate=False)
            return (h @ w2 + b2) * cmask
        B, N, C = x.shape
        B2 = B // 2
        nl = _ln(x[:B2], n1l_g, n1l_b)
        ns = _ln(x[B2:], n1s_g, n1s_b)
        a_large = _attn_branch(nl, w_qkv, w_proj, b_proj, H, C)
        if SMALL_ACTIVE:
            a_small = sum((gumbel_weights[i] * _attn_branch(ns, w_qkv, w_proj, b_proj, H // ALPHA[i], C // ALPHA[i]) for i in range(3)))
            attn_out = jnp.concatenate([a_large, a_small], axis=0)
        else:
            attn_out = jnp.concatenate([a_large, a_large], axis=0)
        x = x + attn_out
        nl2 = _ln(x[:B2], n2l_g, n2l_b)
        ns2 = _ln(x[B2:], n2s_g, n2s_b)
        m_large = _mlp_branch(nl2, w_fc1, b_fc1, w_fc2, b_fc2, C)
        if SMALL_ACTIVE:
            m_small = sum((gumbel_weights[i] * _mlp_branch(ns2, w_fc1, b_fc1, w_fc2, b_fc2, C // ALPHA[i]) for i in range(3)))
            mlp_out = jnp.concatenate([m_large, m_small], axis=0)
        else:
            mlp_out = jnp.concatenate([m_large, m_large], axis=0)
        return x + mlp_out
    h = _L0_tok_ref(x, L0_tok_ln1_g, L0_tok_ln1_b, L0_tok_W, L0_tok_b, L0_tok_ln2_g, L0_tok_ln2_b)
    h = h + _L0_attn_ref(_layernorm(h, axis=-1), L0_attn_position_embeds, L0_attn_Wq, L0_attn_Wk, L0_attn_bk, L0_attn_Wv, L0_attn_bv, L0_attn_r_kernel, L0_attn_r_w_bias, L0_attn_r_r_bias, L0_attn_Wo, L0_attn_bo, L0_attn_gamma, L0_attn_beta)
    h = h + _L0_ffn_ref(_layernorm(h, axis=-1), L0_ffn_gumbel_weights, L0_ffn_n1l_g, L0_ffn_n1l_b, L0_ffn_n1s_g, L0_ffn_n1s_b, L0_ffn_w_qkv, L0_ffn_w_proj, L0_ffn_b_proj, L0_ffn_n2l_g, L0_ffn_n2l_b, L0_ffn_n2s_g, L0_ffn_n2s_b, L0_ffn_w_fc1, L0_ffn_b_fc1, L0_ffn_w_fc2, L0_ffn_b_fc2)
    return h

_drawn_inputs = setup_inputs


def setup_inputs(seed=0):
    import zlib

    import numpy as np

    out = dict(_drawn_inputs(seed))
    spreads = {'L0_tok_ln1_g': (1.0, 0.2),
     'L0_tok_ln1_b': (0.0, 0.1),
     'L0_tok_ln2_g': (1.0, 0.2),
     'L0_tok_ln2_b': (0.0, 0.1),
     'L0_attn_bk': (0.0, 2.0),
     'L0_attn_bv': (0.0, 0.581),
     'L0_attn_bo': (0.0, 0.1),
     'L0_attn_gamma': (1.0, 0.2),
     'L0_attn_beta': (0.0, 0.1),
     'L0_ffn_n1l_g': (1.0, 0.6),
     'L0_ffn_n1l_b': (0.0, 0.8),
     'L0_ffn_n1s_g': (1.0, 0.6),
     'L0_ffn_n1s_b': (0.0, 0.8),
     'L0_ffn_b_proj': (0.0, 0.335),
     'L0_ffn_n2l_g': (1.0, 0.6),
     'L0_ffn_n2l_b': (0.0, 2.0),
     'L0_ffn_n2s_g': (1.0, 0.6),
     'L0_ffn_n2s_b': (0.0, 2.0),
     'L0_ffn_b_fc1': (0.0, 0.8),
     'L0_ffn_b_fc2': (0.0, 0.341)}
    factors = {'L0_attn_position_embeds': 8.0,
     'L0_attn_Wq': 8.0,
     'L0_attn_Wk': 8.0,
     'L0_attn_Wv': 8.0,
     'L0_attn_r_kernel': 8.0,
     'L0_attn_r_w_bias': 8.0,
     'L0_attn_r_r_bias': 8.0,
     'L0_attn_Wo': 3.975,
     'L0_ffn_gumbel_weights': 8.0,
     'L0_ffn_w_qkv': 8.0,
     'L0_ffn_w_proj': 8.0,
     'L0_ffn_w_fc1': 2.802}
    for name, (base, spread) in spreads.items():
        noise = np.random.default_rng([zlib.crc32(name.encode()), seed]).standard_normal(out[name].shape)
        drawn = base * np.exp(spread * noise) if base else spread * noise
        out[name] = jnp.asarray(drawn.astype(out[name].dtype))
    for name, factor in factors.items():
        out[name] = (out[name] * factor).astype(out[name].dtype)
    return out
```

```python
from contextlib import ExitStack

import concourse.bass as bass
from concourse import mybir
from concourse.alu_op_type import AluOpType as ALU

ACT = mybir.ActivationFunctionType
F32 = mybir.dt.float32
AX_X = mybir.AxisListType.X
AX_XY = mybir.AxisListType.XY

P = 128
TOK = 49
ROW = 64
IMAGES = 16
LANES = 2
STEPS = IMAGES // 2 // LANES
LARGE_STEPS = STEPS // 2
D = 192
DC = 96
PATCH = 768
KC = PATCH // P
HEADS = 12
PAIRS = HEADS // 2
DH = 64
DV = D // HEADS
REL = 2 * TOK - 1
RAW = HEADS * REL
SHIFTED = RAW - (TOK - 1)
HID = 4 * D
HC = HID // P
CHUNK = 3
EPS = 1e-5
EPS_ATTN = 1e-9
SCALE = DH ** -0.5
SCALE_FFN = DV ** -0.5
KEEP = (D, D // 2, D // 3)
LN_PER_STEP = 7

ROW_NAMES = ("tok_b", "ln2_g", "ln2_b", "bv", "bo", "gamma", "beta", "b_proj", "b_fc2")
COL6_NAMES = ("ln1_g", "ln1_b", "r_w", "r_r", "bk", "b_fc1")
COL2_NAMES = ("n1l_g", "n1l_b", "n1s_g", "n1s_b", "n2l_g", "n2l_b", "n2s_g", "n2s_b")


def vit_tower(nc, x, w_tok, w_q, w_k, w_v, r_kernel, pos_t, w_o, w_qkv, w_proj, w_fc1, w_fc2,
              rows, cols6, cols2, gumbel, ident_in, parity_in, out):
    with ExitStack() as ctx:
        def sb(name, shape):
            return ctx.enter_context(nc.sbuf_tensor(name, shape, F32))

        def sem(name):
            return ctx.enter_context(nc.semaphore(name))

        def lane_sb(name, shape):
            return [sb(f"{name}{w}", shape) for w in range(LANES)]

        def lane_sem(name):
            return [sem(f"{name}{w}") for w in range(LANES)]

        wtok = sb("wtok", [P, KC, D])
        wtok_g = sb("wtok_g", [P, KC, D])
        wq = sb("wq", [DC, 2, 384])
        wk = sb("wk", [DC, 2, 384])
        wv = sb("wv", [DC, 2, DC])
        rk = sb("rk", [DC, 2, PATCH])
        post = sb("post", [DC, 2, REL])
        rel = sb("rel", [P, PAIRS, REL])
        wo = sb("wo", [DC, 2, D])
        wqkv = sb("wqkv", [DC, 2, 3 * D])
        wproj = [sb("wproj_large", [DC, 2, D]), sb("wproj_small", [DC, 2, D])]
        w1 = sb("w1", [DC, 2, HID])
        w2 = sb("w2", [P, HC, D])
        w2_kept = [sb(f"w2_kept{v}", [P, HC, KEEP[v]]) for v in range(3)]
        row = sb("row", [P, len(ROW_NAMES), D])
        tok_bias = sb("tok_bias", [P, D])
        bproj_small = sb("bproj_small", [P, D])
        b2_small = sb("b2_small", [P, D])
        col6 = sb("col6", [P, len(COL6_NAMES), 6])
        col2 = sb("col2", [DC, len(COL2_NAMES), 2])
        rw_scaled = sb("rw_scaled", [P, PAIRS, 2])
        rr_scaled = sb("rr_scaled", [P, PAIRS, 2])
        gum = sb("gum", [P, 3])
        gum_sum = sb("gum_sum", [P, 3])
        ident = sb("ident", [P, P])
        parity = sb("parity", [DC, 2])
        pool_eps = sb("pool_eps", [P, 2])
        minus_half = sb("minus_half", [P, 1])

        pool_zero = sb("pool_zero", [P, 1])

        def c2(name):
            return col2[:, COL2_NAMES.index(name), :]

        def vec(name):
            return row[:, ROW_NAMES.index(name), :]

        def c6(name):
            return col6[:, COL6_NAMES.index(name), :]

        xt = lane_sb("xt", [P, PATCH])
        xn = lane_sb("xn", [P, PATCH])
        xnT = lane_sb("xnT", [P, KC, P])
        emb = lane_sb("emb", [P, D])
        h = lane_sb("h", [P, D])
        qn = lane_sb("qn", [P, D])
        qn_bo = lane_sb("qn_bo", [P, D])
        h_beta = lane_sb("h_beta", [P, D])
        qnT = lane_sb("qnT", [DC, 2, P])
        qw = lane_sb("qw", [P, PAIRS, P])
        qr = lane_sb("qr", [P, PAIRS, P])
        k1 = lane_sb("k1", [P, PAIRS, P])
        v1 = lane_sb("v1", [P, 2, PAIRS, 2 * DV])
        raw = lane_sb("raw", [P, RAW])
        posS = lane_sb("posS", [P, RAW])
        sc = lane_sb("sc", [P, HEADS * TOK])
        top = lane_sb("top", [P, HEADS])
        den = lane_sb("den", [P, HEADS])
        inv = lane_sb("inv", [P, HEADS])
        prob = lane_sb("prob", [P, PAIRS, 2, ROW])
        probT = lane_sb("probT", [P, PAIRS, P])
        av = lane_sb("av", [P, D])
        avT = lane_sb("avT", [DC, 2, P])
        y = lane_sb("y", [P, D])
        yc = lane_sb("yc", [P, D])
        h1 = lane_sb("h1", [P, D])
        f = lane_sb("f", [P, D])
        f_b = lane_sb("f_b", [P, D])
        nr = lane_sb("nr", [P, D])
        nT = lane_sb("nT", [DC, 2, P])
        q2 = lane_sb("q2", [DC, 2, P])
        k2 = lane_sb("k2", [DC, 2, 2, 2, TOK])
        v2 = lane_sb("v2", [P, 2, PAIRS, 2 * DV])
        f2 = lane_sb("f2", [P, D])
        nr2 = lane_sb("nr2", [P, D])
        n2T = lane_sb("n2T", [DC, 2, P])
        hid = lane_sb("hid", [P, 6, CHUNK, P])
        rest = lane_sb("rest", [P, D])
        rest_b = lane_sb("rest_b", [P, D])
        res = lane_sb("res", [P, D])
        stats = lane_sb("stats", [P, 2, 6])
        mv = lane_sb("mv", [P, LN_PER_STEP, 2])
        var_eps = lane_sb("var_eps", [P, 1])
        rstd = lane_sb("rstd", [P, LN_PER_STEP])
        scratch = [nc.dram_tensor(f"raw_scores{w}", [P, RAW], F32).ap() for w in range(LANES)]

        ps = [ctx.enter_context(nc.psum_tensor(f"ps{w}", [P, 4, 512], F32)) for w in range(LANES)]

        early_loaded = sem("early_loaded")
        late_loaded = sem("late_loaded")
        xt_zeroed = sem("xt_zeroed")
        zeroed_v = sem("zeroed_v")
        zeroed_p = sem("zeroed_p")
        setup_mm = sem("setup_mm")
        setup_v = sem("setup_v")
        setup_p = sem("setup_p")
        dve_chain = sem("dve_chain")
        pool_chain = sem("pool_chain")
        x_loaded = lane_sem("x_loaded")
        xn_ready = lane_sem("xn_ready")
        xT_mm = lane_sem("xT_mm")
        xT_ready = lane_sem("xT_ready")
        tok_mm = lane_sem("tok_mm")
        h_ready = lane_sem("h_ready")
        qn_ready = lane_sem("qn_ready")
        qnT_mm = lane_sem("qnT_mm")
        qnT_ready = lane_sem("qnT_ready")
        q_mm = lane_sem("q_mm")
        qr_ready = lane_sem("qr_ready")
        qw_ready = lane_sem("qw_ready")
        k_mm = lane_sem("k_mm")
        k_ready = lane_sem("k_ready")
        pos_mm = lane_sem("pos_mm")
        raw_ready = lane_sem("raw_ready")
        raw_stored = lane_sem("raw_stored")
        pos_loaded = lane_sem("pos_loaded")
        score_mm = [lane_sem("score_mm_a"), lane_sem("score_mm_b")]
        sc_ready = [lane_sem("sc_ready_a"), lane_sem("sc_ready_b")]
        prob_ready = [lane_sem("prob_ready_a"), lane_sem("prob_ready_b")]
        v_mm = [lane_sem("v_mm_a"), lane_sem("v_mm_b")]
        v_ready = [lane_sem("v_ready_a"), lane_sem("v_ready_b")]
        pT_mm = [lane_sem("pT_mm_a"), lane_sem("pT_mm_b")]
        pT_ready_act = [lane_sem("pT_act_a"), lane_sem("pT_act_b")]
        pT_ready_dve = [lane_sem("pT_dve_a"), lane_sem("pT_dve_b")]
        pv_mm = [lane_sem("pv_mm_a"), lane_sem("pv_mm_b")]
        av_ready = [lane_sem("av_ready_a"), lane_sem("av_ready_b")]
        avT_mm = [lane_sem("avT_mm_a"), lane_sem("avT_mm_b")]
        avT_ready = [lane_sem("avT_ready_a"), lane_sem("avT_ready_b")]
        o_mm = [lane_sem("o_mm_a"), lane_sem("o_mm_b")]
        var_ready = lane_sem("var_ready")
        rstd_ready = lane_sem("rstd_ready")
        qn_bo_ready = lane_sem("qn_bo_ready")
        h_beta_ready = lane_sem("h_beta_ready")
        h1_ready = lane_sem("h1_ready")
        f_ready = lane_sem("f_ready")
        f_b_ready = lane_sem("f_b_ready")
        nr_ready = lane_sem("nr_ready")
        nT_mm = lane_sem("nT_mm")
        nT_ready = lane_sem("nT_ready")
        q2_mm = lane_sem("q2_mm")
        q2_ready = lane_sem("q2_ready")
        k2_mm = lane_sem("k2_mm")
        k2_ready = lane_sem("k2_ready")
        f2_ready = lane_sem("f2_ready")
        nr2_ready = lane_sem("nr2_ready")
        n2T_mm = lane_sem("n2T_mm")
        n2T_ready = lane_sem("n2T_ready")
        fc1_mm = lane_sem("fc1_mm")
        gelu_ready = lane_sem("gelu_ready")
        fc2_mm = lane_sem("fc2_mm")
        rest_ready = lane_sem("rest_ready")
        res_ready = lane_sem("res_ready")
        res_free = lane_sem("res_free")

        BANKS = (2, 3, 1)
        EARLY = 16 * 6
        LATE = 16 * (12 + 6 + 2)
        ZEROED_V = 1
        ZEROED_P = 1

        def chunks(small):
            return [(v, c) for v in range(3 if small else 1) for c in range(0, HC, CHUNK)]

        def chunk_count(n, j, small):
            large = len(chunks(False))
            if not small:
                return n * large + (j + 1)
            per = len(chunks(True))
            return n * per + (LARGE_STEPS * (large - per) + j + 1)

        def valid(ap):
            return ap.rearrange("p (b t) -> p b t", b=2)[:, :, 0:TOK]

        block = ctx.enter_context(nc.Block())

        @block.sync
        def _(sp):
            def load_x(n, w):
                for b in range(2):
                    sp.dma_start(xt[w][b * ROW:b * ROW + TOK, :], x[n, w, b]).then_inc(x_loaded[w], 16)

            for w in range(LANES):
                sp.wait_ge(xt_zeroed, w + 1)
                load_x(0, w)
            for dst, src in ((wq, w_q), (wk, w_k)):
                if dst is wq:
                    sp.wait_ge(zeroed_p, ZEROED_P)
                for g in range(4):
                    r, c = (g % 2) * 48, (g % 2) * D
                    sp.dma_start(dst[r:r + 48, g // 2, c:c + D], src[g]).then_inc(late_loaded, 16)
            for g in range(4):
                r = (g % 2) * 48
                sp.dma_start(wv[r:r + 48, g // 2, r:r + 48], w_v[g]).then_inc(late_loaded, 16)

            def step(n, last):
                for w in range(LANES):
                    sp.wait_ge(raw_ready[w], n + 1)
                    sp.dma_start(scratch[w][0:ROW + TOK, :], raw[w][0:ROW + TOK, :]).then_inc(raw_stored[w], 16)
                    sp.wait_ge(raw_stored[w], 16 * n + 16)
                    for b in range(2):
                        skewed = bass.AP(scratch[w].tensor, b * ROW * RAW + TOK - 1,
                                         [[RAW - 1, TOK], [1, SHIFTED]])
                        sp.dma_start(posS[w][b * ROW:b * ROW + TOK, 0:SHIFTED],
                                     skewed).then_inc(pos_loaded[w], 16)
                if not last:
                    for w in range(LANES):
                        sp.wait_ge(xn_ready[w], n + 1)
                        load_x(n + 1, w)
                for w in range(LANES):
                    sp.wait_ge(res_ready[w], n + 1)
                    for b in range(2):
                        sp.dma_start(out[n, w, b], res[w][b * ROW:b * ROW + TOK, :]).then_inc(res_free[w], 16)

            with sp.Fori(0, STEPS - 1) as n:
                step(n, False)
            step(STEPS - 1, True)
            for w in range(LANES):
                sp.wait_ge(res_free[w], 32 * STEPS + 32)

        @block.gpsimd
        def _(pool):
            chain = [0]

            def link(ins):
                chain[0] += 1
                ins.then_inc(pool_chain, 1)
                pool.wait_ge(pool_chain, chain[0])

            def restart():
                pool.sem_clear(pool_chain)
                chain[0] = 0

            pool.memset(wq[:], 0.0)
            pool.memset(wk[:], 0.0)
            pool.memset(wv[:], 0.0).then_inc(zeroed_p, 1)

            def rsqrt(n, w, i):
                eps = pool_eps[:, 1:2] if i == 3 else pool_eps[:, 0:1]
                pool.wait_ge(var_ready[w], n * LN_PER_STEP + (i + 1))
                link(pool.tensor_tensor(var_eps[w][:], mv[w][:, i, 1:2], eps, ALU.add))
                pool.tensor_tensor(rstd[w][:, i:i + 1], var_eps[w][:], minus_half[:],
                                   ALU.pow).then_inc(rstd_ready[w], 1)

            def step(n, small):
                restart()
                lanes = range(LANES)
                for i in range(3):
                    for w in lanes:
                        rsqrt(n, w, i)
                for w in lanes:
                    pool.wait_ge(h_ready[w], n + 1)
                    pool.tensor_tensor(h_beta[w][:], h[w][:], vec("beta"), ALU.add).then_inc(h_beta_ready[w], 1)
                    pool.wait_ge(qn_ready[w], n + 1)
                    pool.tensor_tensor(qn_bo[w][:], qn[w][:], vec("bo"), ALU.add).then_inc(qn_bo_ready[w], 1)
                for i in range(3, 6):
                    for w in lanes:
                        rsqrt(n, w, i)
                for w in lanes:
                    pool.wait_ge(f_ready[w], n + 1)
                    pool.tensor_tensor(f_b[w][:], f[w][:], bproj_small[:] if small else vec("b_proj"),
                                       ALU.add).then_inc(f_b_ready[w], 1)
                for w in lanes:
                    rsqrt(n, w, 6)
                for w in lanes:
                    pool.wait_ge(f2_ready[w], n + 1)
                    link(pool.tensor_tensor(rest[w][:], h1[w][:], f2[w][:], ALU.add))
                    pool.tensor_tensor(rest_b[w][:], rest[w][:], b2_small[:] if small else vec("b_fc2"),
                                       ALU.add).then_inc(rest_ready[w], 1)

            def small_setup():
                restart()

                def times(dst, src, g):
                    link(pool.tensor_scalar(dst, src, g, 1.0, ALU.mult, ALU.mult))

                link(pool.tensor_tensor(gum_sum[:, 0:1], gum[:, 0:1], pool_zero[:], ALU.add))
                link(pool.tensor_tensor(gum_sum[:, 1:2], gum_sum[:, 0:1], gum[:, 1:2], ALU.add))
                link(pool.tensor_tensor(gum_sum[:, 2:3], gum_sum[:, 1:2], gum[:, 2:3], ALU.add))
                pool.wait_ge(late_loaded, LATE)
                cuts = ((0, KEEP[2], 2), (KEEP[2], KEEP[1], 1), (KEEP[1], D, 0))
                for a, b, g in cuts:
                    times(bproj_small[:, a:b], vec("b_proj")[:, a:b], gum_sum[:, g:g + 1])
                    times(b2_small[:, a:b], vec("b_fc2")[:, a:b], gum_sum[:, g:g + 1])
                for a, b, g in cuts:
                    times(wproj[1][0:KEEP[2], 0, a:b], wproj[0][0:KEEP[2], 0, a:b], gum_sum[0:KEEP[2], g:g + 1])
                for a, b, g in ((0, KEEP[1], 1), (KEEP[1], D, 0)):
                    times(wproj[1][KEEP[2]:DC, 0, a:b], wproj[0][KEEP[2]:DC, 0, a:b], gum_sum[KEEP[2]:DC, g:g + 1])
                times(wproj[1][:, 1, :], wproj[0][:, 1, :], gum_sum[0:DC, 0:1])
                for v in range(2):
                    times(w2_kept[v][:], w2[:, :, 0:KEEP[v]], gum[:, v:v + 1])
                pool.tensor_scalar(w2_kept[2][:], w2[:, :, 0:KEEP[2]], gum[:, 2:3], 1.0, ALU.mult,
                                   ALU.mult).then_inc(setup_p, 1)

            pool.wait_ge(early_loaded, EARLY)
            pool.wait_ge(zeroed_v, ZEROED_V)
            with pool.Fori(0, LARGE_STEPS) as n:
                step(n, False)
            small_setup()
            with pool.Fori(LARGE_STEPS, STEPS) as n:
                step(n, True)

        @block.scalar
        def _(act):
            lanes = range(LANES)
            ones = ((ident, ident_in), (col6, cols6), (wtok, w_tok), (gum, None), (row, None), (parity, parity_in))
            for dst, src in ones:
                if dst is gum:
                    src = bass.AP(gumbel.tensor, 0, [[0, P], [1, 3]])
                if dst is row:
                    src = bass.AP(rows.tensor, 0, [[0, P], [D, len(ROW_NAMES)], [1, D]])
                act.dma_start(dst[:], src).then_inc(early_loaded, 16)
            for dst, src in ((col2, cols2), (post, pos_t), (rk, r_kernel), (wo, w_o), (wqkv, w_qkv),
                             (wproj[0], w_proj)):
                act.dma_start(dst[:], src).then_inc(late_loaded, 16)
            act.wait_ge(zeroed_v, ZEROED_V)

            def transposed_probs(n, w, a):
                act.wait_ge(pT_mm[a][w], n + 1)
                act.activation(probT[w][:, 0:3, :], ps[w][:, 0, 0:384], ACT.Copy).then_inc(pT_ready_act[a][w], 1)

            def exp_scores(n, w, a):
                act.wait_ge(sc_ready[a][w], n + 1)
                if a == 0:
                    dst = prob[w][:, :, :, 0:TOK].rearrange("p m r t -> p r m t")
                    src = sc[w][:].rearrange("p (r m t) -> p r m t", r=2, t=TOK)
                else:
                    dst = prob[w][:, :, :, 0:TOK].rearrange("p m r t -> p (m r) t")
                    src = sc[w][:].rearrange("p (n t) -> p n t", t=TOK)
                act.activation(dst, src, ACT.Exp).then_inc(prob_ready[a][w], 1)

            def transposed_av(n, w, a):
                act.wait_ge(avT_mm[a][w], n + 1)
                act.activation(avT[w][:], ps[w][0:DC, 3, 0:2 * P], ACT.Copy).then_inc(avT_ready[a][w], 1)

            def affine_columns(n, w, done, dst, gain, shift, ready):
                act.wait_ge(done[w], n + 1)
                for c in range(2):
                    last = act.activation(dst[w][:, c, :], ps[w][0:DC, 1, c * P:(c + 1) * P], ACT.Identity,
                                          scale=gain[:, c:c + 1], bias=shift[:, c:c + 1])
                last.then_inc(ready[w], 1)

            def step(n, small):
                size = "s" if small else "l"
                for w in lanes:
                    act.wait_ge(xT_mm[w], n + 1)
                    act.activation(xnT[w][:, 0:4, :], ps[w][:, 0, :], ACT.Copy)
                    act.activation(xnT[w][:, 4:6, :], ps[w][:, 1, 0:256], ACT.Copy).then_inc(xT_ready[w], 1)
                for w in lanes:
                    act.wait_ge(qnT_mm[w], n + 1)
                    act.activation(qnT[w][:], ps[w][0:DC, 3, 0:2 * P], ACT.Copy).then_inc(qnT_ready[w], 1)
                for w in lanes:
                    act.wait_ge(k_mm[w], n + 1)
                    for m in range(PAIRS):
                        c, o = m // 3, (m % 3) * 2 * TOK
                        last = act.activation(valid(k1[w][:, m, :]),
                                              ps[w][:, 2 + c, o:o + 2 * TOK].rearrange("p (b t) -> p b t", b=2),
                                              ACT.Identity, bias=c6("bk")[:, m:m + 1])
                    last.then_inc(k_ready[w], 1)
                for w in lanes:
                    act.wait_ge(pos_mm[w], n + 1)
                    for r in range(2):
                        last = act.activation(raw[w][:, r * RAW // 2:(r + 1) * RAW // 2].rearrange("p (k s) -> p k s", k=2),
                                              ps[w][:, 2 * r:2 * r + 2, 0:3 * REL], ACT.Copy)
                    last.then_inc(raw_ready[w], 1)
                for w in lanes:
                    exp_scores(n, w, 0)
                for w in lanes:
                    transposed_probs(n, w, 0)
                for w in lanes:
                    transposed_av(n, w, 0)
                for w in lanes:
                    affine_columns(n, w, nT_mm, nT, c2(f"n1{size}_g"), c2(f"n1{size}_b"), nT_ready)
                for w in lanes:
                    exp_scores(n, w, 1)
                for w in lanes:
                    transposed_probs(n, w, 1)
                for w in lanes:
                    transposed_av(n, w, 1)
                for w in lanes:
                    affine_columns(n, w, n2T_mm, n2T, c2(f"n2{size}_g"), c2(f"n2{size}_b"), n2T_ready)
                for j, (v, c) in enumerate(chunks(small)):
                    for w in lanes:
                        act.wait_ge(fc1_mm[w], chunk_count(n, j, small))
                        for i in range(CHUNK):
                            last = act.activation(
                                valid(hid[w][:, j, i, :]),
                                ps[w][:, BANKS[j % 3], i * 2 * TOK:(i + 1) * 2 * TOK].rearrange("p (b t) -> p b t", b=2),
                                ACT.Gelu, bias=c6("b_fc1")[:, c + i:c + i + 1])
                        last.then_inc(gelu_ready[w], 1)

            act.dma_start(w1[:], w_fc1).then_inc(late_loaded, 16)
            act.dma_start(w2[:], w_fc2).then_inc(late_loaded, 16)
            act.wait_ge(early_loaded, EARLY)
            act.wait_ge(late_loaded, LATE)
            with act.Fori(0, LARGE_STEPS) as n:
                step(n, False)
            with act.Fori(LARGE_STEPS, STEPS) as n:
                step(n, True)

        @block.vector
        def _(dve):
            lanes = range(LANES)
            chain = [0]

            def link(ins):
                chain[0] += 1
                ins.then_inc(dve_chain, 1)
                dve.wait_ge(dve_chain, chain[0])

            def restart():
                dve.sem_clear(dve_chain)
                chain[0] = 0

            for w in lanes:
                dve.memset(xt[w][:], 0.0).then_inc(xt_zeroed, 1)
            dve.memset(pool_eps[:, 0:1], EPS)
            dve.memset(pool_eps[:, 1:2], EPS_ATTN)
            dve.memset(pool_zero[:], 0.0)
            dve.memset(minus_half[:], -0.5)
            for w in lanes:
                dve.memset(res[w][:], 0.0).then_inc(res_free[w], 32)
                for t in (qw, qr, k1, v1, v2, posS, prob, q2, hid):
                    dve.memset(t[w][:], 0.0)
                last = dve.memset(ps[w][:, 1:4, :], 0.0)
            last.then_inc(zeroed_v, 1)
            dve.wait_ge(early_loaded, EARLY)
            for c in range(KC):
                dve.tensor_scalar(wtok_g[:, c, :], wtok[:, c, :], c6("ln1_g")[:, c:c + 1], None, ALU.mult)
            for dst, name in ((rw_scaled, "r_w"), (rr_scaled, "r_r")):
                dve.tensor_scalar(dst[:], c6(name).unsqueeze(2).to_broadcast([P, PAIRS, 2]), SCALE, None, ALU.mult)
            dve.wait_ge(setup_mm, 1)
            dve.tensor_tensor(tok_bias[:], ps[0][:, 0, 0:D], vec("tok_b"), ALU.add).then_inc(setup_v, 1)

            def relative_keys():
                dve.wait_ge(setup_mm, 2)
                for r in range(2):
                    last = dve.tensor_copy(rel[:, 3 * r:3 * r + 3, :], ps[0][:, r, 0:3 * REL].rearrange("p (m t) -> p m t", m=3))
                last.then_inc(setup_v, 1)

            def moments(n, w, i, src):
                k = src.shape[1] // 384 or 1
                size = src.shape[1] // k
                for j in range(k):
                    last = dve.bn_stats(stats[w][:, j, :], src[:, j * size:(j + 1) * size])
                link(last)
                dve.bn_aggr(mv[w][:, i, :], stats[w][:, 0:k, :]).then_inc(var_ready[w], 1)

            def mean(w, i):
                return mv[w][:, i, 0:1]

            def inv_dev(w, i):
                return rstd[w][:, i:i + 1]

            def rstd_done(n, w, i):
                dve.wait_ge(rstd_ready[w], n * LN_PER_STEP + (i + 1))

            def normalise(n, w, i, src, dst):
                rstd_done(n, w, i)
                return dve.tensor_scalar(dst, src, mean(w, i), inv_dev(w, i), ALU.subtract, ALU.mult)

            def normalise_affine(n, w, i, src, gain, shift, dst):
                rstd_done(n, w, i)
                link(dve.scalar_tensor_tensor(out=yc[w][:], in0=src, scalar=mean(w, i), in1=gain,
                                              op0=ALU.subtract, op1=ALU.mult))
                return dve.scalar_tensor_tensor(out=dst, in0=yc[w][:], scalar=inv_dev(w, i), in1=shift,
                                                op0=ALU.mult, op1=ALU.add)

            def per_head(ap):
                return ap.unsqueeze(2).to_broadcast([P, HEADS, TOK])

            def softmax_front(n, w, a):
                flat = sc[w][:].rearrange("p (n t) -> p n t", t=TOK)
                if a == 0:
                    dve.wait_ge(pos_loaded[w], 32 * n + 32)
                    dve.wait_ge(score_mm[0][w], n + 1)
                    link(dve.tensor_tensor(
                        sc[w][:].rearrange("p (r m t) -> p r m t", r=2, t=TOK),
                        ps[w][:, 2:4, 0:PAIRS * TOK].rearrange("p r (m t) -> p r m t", t=TOK),
                        posS[w][:].rearrange("p (r m t) -> p r m t", r=2, t=REL)[:, :, :, 0:TOK], ALU.add))
                    src, top_src = flat, flat
                    top_dst = top[w][:]
                else:
                    dve.wait_ge(score_mm[1][w], n + 1)
                    src = ps[w][:, 1:4, 0:4 * TOK].rearrange("p g (q t) -> p g q t", t=TOK)
                    top_src, top_dst = src, top[w][:].rearrange("p (g q) -> p g q", g=3)
                link(dve.tensor_reduce(top_dst, top_src, AX_X, ALU.max))
                if a == 0:
                    last = dve.tensor_tensor(flat, flat, per_head(top[w][:]), ALU.subtract)
                else:
                    last = dve.tensor_tensor(
                        sc[w][:].rearrange("p (g q t) -> p g q t", g=3, t=TOK), src,
                        top[w][:].rearrange("p (g q) -> p g q", g=3).unsqueeze(3).to_broadcast([P, 3, 4, TOK]),
                        ALU.subtract)
                last.then_inc(sc_ready[a][w], 1)

            def values(n, w, a):
                dst = (v1, v2)[a][w]
                dve.wait_ge(v_mm[a][w], n + 1)
                for r in range(2):
                    rows_ = slice(r * ROW, (r + 1) * ROW)
                    o = dst[rows_, :, :, r * DV:(r + 1) * DV]
                    i = ps[w][rows_, 0, 0:D].rearrange("p (b m d) -> p b m d", b=2, d=DV)
                    if a == 0:
                        bias = vec("bv")[rows_].rearrange("p (m r d) -> p m r d", r=2, d=DV)[:, :, r, :]
                        last = dve.tensor_tensor(o, i, bias.unsqueeze(1).to_broadcast([ROW, 2, PAIRS, DV]), ALU.add)
                    else:
                        last = dve.tensor_copy(o, i)
                last.then_inc(v_ready[a][w], 1)

            def denominators(n, w, a):
                dve.wait_ge(prob_ready[a][w], n + 1)
                link(dve.tensor_reduce(den[w][:], prob[w][:, :, :, 0:TOK].rearrange("p m r t -> p (m r) t"),
                                       AX_X, ALU.add))
                link(dve.reciprocal(inv[w][:], den[w][:]))

            def transposed_probs(n, w, a):
                dve.wait_ge(pT_mm[a][w], n + 1)
                dve.tensor_copy(probT[w][:, 3:6, :], ps[w][:, 1, 0:384].rearrange("p (m t) -> p m t", m=3)).then_inc(
                    pT_ready_dve[a][w], 1)

            def attended(n, w, a):
                dve.wait_ge(pv_mm[a][w], n + 1)
                dve.tensor_tensor(av[w][:].rearrange("p (n d) -> p n d", d=DV),
                                  ps[w][:, 2, 0:D].rearrange("p (n d) -> p n d", d=DV),
                                  inv[w][:].unsqueeze(2).to_broadcast([P, HEADS, DV]),
                                  ALU.mult).then_inc(av_ready[a][w], 1)

            def step(n, small):
                restart()
                for w in lanes:
                    dve.wait_ge(x_loaded[w], 32 * n + 32)
                    moments(n, w, 0, xt[w][:])
                for w in lanes:
                    normalise(n, w, 0, xt[w][:], xn[w][:]).then_inc(xn_ready[w], 1)
                for w in lanes:
                    dve.wait_ge(tok_mm[w], n + 1)
                    link(dve.tensor_tensor(emb[w][:], ps[w][:, 2, 0:D], tok_bias[:], ALU.add))
                    moments(n, w, 1, emb[w][:])
                for w in lanes:
                    normalise_affine(n, w, 1, emb[w][:], vec("ln2_g"), vec("ln2_b"), h[w][:]).then_inc(h_ready[w], 1)
                    dve.wait_ge(h_ready[w], n + 1)
                    moments(n, w, 2, h[w][:])
                for w in lanes:
                    normalise(n, w, 2, h[w][:], qn[w][:]).then_inc(qn_ready[w], 1)
                for w in lanes:
                    dve.wait_ge(q_mm[w], n + 1)
                    for dst, bias, ready in ((qr, rr_scaled, qr_ready), (qw, rw_scaled, qw_ready)):
                        for c in range(2):
                            last = dve.scalar_tensor_tensor(
                                out=dst[w][:, 3 * c:3 * c + 3, :].rearrange("p m (b t) -> p (m b) t", b=2)[:, :, 0:TOK],
                                in0=ps[w][:, c, 0:6 * TOK].rearrange("p (q t) -> p q t", t=TOK), scalar=SCALE,
                                in1=bias[:, 3 * c:3 * c + 3, :].rearrange("p m b -> p (m b)").unsqueeze(2).to_broadcast([P, 6, TOK]),
                                op0=ALU.mult, op1=ALU.add)
                        last.then_inc(ready[w], 1)
                for w in lanes:
                    values(n, w, 0)
                for w in lanes:
                    softmax_front(n, w, 0)
                for w in lanes:
                    denominators(n, w, 0)
                    transposed_probs(n, w, 0)
                for w in lanes:
                    attended(n, w, 0)
                for w in lanes:
                    dve.wait_ge(qn_bo_ready[w], n + 1)
                    dve.wait_ge(o_mm[0][w], n + 1)
                    link(dve.tensor_tensor(y[w][:], ps[w][:, 0, 0:D], qn_bo[w][:], ALU.add))
                    moments(n, w, 3, y[w][:])
                for w in lanes:
                    dve.wait_ge(h_beta_ready[w], n + 1)
                    normalise_affine(n, w, 3, y[w][:], vec("gamma"), h_beta[w][:], h1[w][:]).then_inc(h1_ready[w], 1)
                    dve.wait_ge(h1_ready[w], n + 1)
                    moments(n, w, 4, h1[w][:])
                for w in lanes:
                    normalise(n, w, 4, h1[w][:], f[w][:]).then_inc(f_ready[w], 1)
                    dve.wait_ge(f_ready[w], n + 1)
                    moments(n, w, 5, f[w][:])
                for w in lanes:
                    normalise(n, w, 5, f[w][:], nr[w][:]).then_inc(nr_ready[w], 1)
                for w in lanes:
                    dve.wait_ge(q2_mm[w], n + 1)
                    dve.tensor_scalar(q2[w][:].rearrange("p c (b t) -> p c b t", b=2)[:, :, :, 0:TOK],
                                      ps[w][0:DC, 2, 0:4 * TOK].rearrange("p (c b t) -> p c b t", c=2, b=2),
                                      SCALE_FFN, None, ALU.mult).then_inc(q2_ready[w], 1)
                    dve.wait_ge(k2_mm[w], n + 1)
                    for r in range(2):
                        last = dve.tensor_scalar(k2[w][:, :, :, r, :],
                                                 ps[w][0:DC, 3, 0:4 * TOK].rearrange("p (c b t) -> p c b t", c=2, b=2),
                                                 parity[:, r:r + 1], None, ALU.mult)
                    last.then_inc(k2_ready[w], 1)
                for w in lanes:
                    values(n, w, 1)
                    softmax_front(n, w, 1)
                for w in lanes:
                    denominators(n, w, 1)
                    transposed_probs(n, w, 1)
                for w in lanes:
                    attended(n, w, 1)
                for w in lanes:
                    dve.wait_ge(f_b_ready[w], n + 1)
                    dve.wait_ge(o_mm[1][w], n + 1)
                    dve.tensor_tensor(f2[w][:], ps[w][:, 0, 0:D], f_b[w][:], ALU.add).then_inc(f2_ready[w], 1)
                    dve.wait_ge(f2_ready[w], n + 1)
                    moments(n, w, 6, f2[w][:])
                for w in lanes:
                    normalise(n, w, 6, f2[w][:], nr2[w][:]).then_inc(nr2_ready[w], 1)
                for w in lanes:
                    dve.wait_ge(rest_ready[w], n + 1)
                    dve.wait_ge(res_free[w], 32 * n + 32)
                    dve.wait_ge(fc2_mm[w], n + 1)
                    dve.tensor_tensor(res[w][:], ps[w][:, 0, 0:D], rest_b[w][:], ALU.add).then_inc(res_ready[w], 1)

            relative_keys()
            with dve.Fori(0, LARGE_STEPS) as n:
                step(n, False)
            with dve.Fori(LARGE_STEPS, STEPS) as n:
                step(n, True)

        @block.tensor
        def _(pe):
            lanes = range(LANES)

            def features(src, w):
                def into(bank):
                    for c in range(2):
                        last = pe.transpose(ps[w][0:DC, bank, c * P:(c + 1) * P], src[w][:, c * DC:(c + 1) * DC], ident[:])
                    return last
                return into

            def every_other(weights, r):
                return weights.rearrange("p (m r d) -> p m r d", r=2, d=DV)[:, :, r, :]

            def tokens(srcT, w, c):
                return valid(srcT[w][:, c, :])

            def back(n, w, a, weights):
                vals = (v1, v2)[a][w]

                def transposes():
                    pe.wait_ge(prob_ready[a][w], n + 1)
                    pe.wait_ge(v_ready[a][w], n + 1)
                    for m in range(PAIRS):
                        last = pe.transpose(ps[w][:, m // 3, (m % 3) * P:(m % 3 + 1) * P],
                                            prob[w][:, m, :, :].rearrange("p r t -> p (r t)"), ident[:])
                    last.then_inc(pT_mm[a][w], 1)

                def attend():
                    pe.wait_ge(pT_ready_act[a][w], n + 1)
                    pe.wait_ge(pT_ready_dve[a][w], n + 1)
                    for b in range(2):
                        for m in range(PAIRS):
                            last = pe.matmul(ps[w][b * ROW:b * ROW + TOK, 2, m * 32:(m + 1) * 32],
                                             probT[w][:, m, b * ROW:b * ROW + TOK], vals[:, b, m, :],
                                             start=True, stop=True)
                    last.then_inc(pv_mm[a][w], 1)

                def turn():
                    pe.wait_ge(av_ready[a][w], n + 1)
                    features(av, w)(3).then_inc(avT_mm[a][w], 1)

                def project():
                    pe.wait_ge(avT_ready[a][w], n + 1)
                    for c in range(2):
                        last = pe.matmul(ps[w][:, 0, 0:D], avT[w][:, c, :], weights[:, c, :],
                                         start=(c == 0), stop=(c == 1))
                    last.then_inc(o_mm[a][w], 1)

                return transposes, attend, turn, project

            def in_stages(all_lanes):
                for stage in range(len(all_lanes[0])):
                    for w in lanes:
                        all_lanes[w][stage]()

            def fc1(n, w, j, v, c, small):
                if j == 0:
                    pe.wait_ge(n2T_ready[w], n + 1)
                if j >= 3:
                    pe.wait_ge(gelu_ready[w], chunk_count(n, j - 3, small))
                keep = KEEP[v]
                for i in range(CHUNK):
                    dst = ps[w][:, BANKS[j % 3], i * 2 * TOK:(i + 1) * 2 * TOK]
                    cols = slice((c + i) * P, (c + i + 1) * P)
                    for kc in range(2 if keep > DC else 1):
                        k = min(keep, DC)
                        last = pe.matmul(dst, w1[0:k, kc, cols], valid(n2T[w][0:k, kc, :]),
                                         start=(kc == 0), stop=(kc == 1 or keep <= DC))
                last.then_inc(fc1_mm[w], 1)

            def fc2(n, w, j, v, c, small):
                pe.wait_ge(gelu_ready[w], chunk_count(n, j, small))
                weights = w2_kept[v] if small else w2
                for i in range(CHUNK):
                    first = j == 0 and i == 0
                    final = j == len(chunks(small)) - 1 and i == CHUNK - 1
                    last = pe.matmul(ps[w][:, 0, 0:KEEP[v]], hid[w][:, j, i, :], weights[:, c + i, :],
                                     start=first, stop=final, skip_group_check=True)
                if final:
                    last.then_inc(fc2_mm[w], 1)

            def step(n, small):
                for w in lanes:
                    pe.wait_ge(xn_ready[w], n + 1)
                    for c in range(KC):
                        last = pe.transpose(ps[w][:, c // 4, (c % 4) * P:(c % 4 + 1) * P],
                                            xn[w][:, c * P:(c + 1) * P], ident[:])
                    last.then_inc(xT_mm[w], 1)
                for w in lanes:
                    pe.wait_ge(xT_ready[w], n + 1)
                    for c in range(KC):
                        last = pe.matmul(ps[w][:, 2, 0:D], xnT[w][:, c, :], wtok_g[:, c, :],
                                         start=(c == 0), stop=(c == KC - 1))
                    last.then_inc(tok_mm[w], 1)
                for w in lanes:
                    pe.wait_ge(qn_ready[w], n + 1)
                    features(qn, w)(3).then_inc(qnT_mm[w], 1)
                for w in lanes:
                    pe.wait_ge(qnT_ready[w], n + 1)
                    for bank, weights, done in ((0, wq, q_mm), (2, wk, k_mm)):
                        for m in range(PAIRS):
                            o = (m % 3) * 2 * TOK
                            last = pe.matmul(ps[w][:, bank + m // 3, o:o + 2 * TOK],
                                             weights[:, m // 3, (m % 3) * P:(m % 3 + 1) * P],
                                             tokens(qnT, w, m // 3), start=True, stop=True)
                        last.then_inc(done[w], 1)
                for w in lanes:
                    pe.wait_ge(qr_ready[w], n + 1)
                    pe.wait_ge(qw_ready[w], n + 1)
                    pe.wait_ge(k_ready[w], n + 1)
                    for m in range(PAIRS):
                        for r in range(2):
                            half = slice(r * DH, (r + 1) * DH)
                            last = pe.matmul(ps[w][:, 2 * r + m // 3, (m % 3) * REL:(m % 3 + 1) * REL],
                                             qr[w][half, m, :], rel[half, m, :], start=True, stop=True)
                    last.then_inc(pos_mm[w], 1)
                for w in lanes:
                    pe.wait_ge(raw_ready[w], n + 1)
                    for b in range(2):
                        for r in range(2):
                            for c in range(2):
                                last = pe.matmul(ps[w][r * ROW:(r + 1) * ROW, 0, b * DC + c * 48:b * DC + (c + 1) * 48],
                                                 qnT[w][:, c, b * ROW:(b + 1) * ROW], every_other(wv[:, c, :], r),
                                                 start=True, stop=True)
                    last.then_inc(v_mm[0][w], 1)
                    for m in range(PAIRS):
                        for b in range(2):
                            cols = slice(b * ROW, b * ROW + TOK)
                            for r in range(2):
                                half = slice(r * DH, (r + 1) * DH)
                                last = pe.matmul(ps[w][b * ROW:b * ROW + TOK, 2 + r, m * TOK:(m + 1) * TOK],
                                                 qw[w][half, m, cols], k1[w][half, m, cols], start=True, stop=True)
                    last.then_inc(score_mm[0][w], 1)
                in_stages([back(n, w, 0, wo) for w in lanes])
                for w in lanes:
                    pe.wait_ge(nr_ready[w], n + 1)
                    features(nr, w)(1).then_inc(nT_mm[w], 1)
                for w in lanes:
                    pe.wait_ge(nT_ready[w], n + 1)
                    for bank, first, done in ((2, 0, q2_mm), (3, D, k2_mm)):
                        for c in range(2):
                            for kc in range(2):
                                cols = wqkv[:, kc, first + c * DC:first + (c + 1) * DC]
                                last = pe.matmul(ps[w][0:DC, bank, c * 2 * TOK:(c + 1) * 2 * TOK], cols,
                                                 tokens(nT, w, kc), start=(kc == 0), stop=(kc == 1))
                        last.then_inc(done[w], 1)
                    for b in range(2):
                        for r in range(2):
                            for c in range(2):
                                last = pe.matmul(ps[w][r * ROW:(r + 1) * ROW, 0, b * DC:(b + 1) * DC],
                                                 nT[w][:, c, b * ROW:(b + 1) * ROW],
                                                 every_other(wqkv[:, c, 2 * D:3 * D], r),
                                                 start=(c == 0), stop=(c == 1))
                    last.then_inc(v_mm[1][w], 1)
                for w in lanes:
                    pe.wait_ge(q2_ready[w], n + 1)
                    pe.wait_ge(k2_ready[w], n + 1)
                    for c in range(2):
                        for b in range(2):
                            for g in range(3):
                                part = slice(g * 32, (g + 1) * 32)
                                last = pe.matmul(ps[w][b * ROW:b * ROW + TOK, 1 + g, c * 2 * TOK:(c + 1) * 2 * TOK],
                                                 q2[w][part, c, b * ROW:b * ROW + TOK],
                                                 k2[w][part, c, b, :, :].rearrange("p r t -> p (r t)"),
                                                 start=True, stop=True)
                    last.then_inc(score_mm[1][w], 1)
                in_stages([back(n, w, 1, wproj[small]) for w in lanes])
                for w in lanes:
                    pe.wait_ge(nr2_ready[w], n + 1)
                    features(nr2, w)(1).then_inc(n2T_mm[w], 1)
                todo = chunks(small)
                for j in range(len(todo) + 2):
                    for w in lanes:
                        if j < len(todo):
                            fc1(n, w, j, *todo[j], small)
                        if j >= 2:
                            fc2(n, w, j - 2, *todo[j - 2], small)

            pe.wait_ge(zeroed_v, ZEROED_V)
            pe.wait_ge(early_loaded, EARLY)
            for c in range(KC):
                last = pe.matmul(ps[0][:, 0, 0:D], c6("ln1_b")[:, c:c + 1].to_broadcast([P, P]), wtok[:, c, :],
                                 start=(c == 0), stop=(c == KC - 1))
            last.then_inc(setup_mm, 1)
            pe.wait_ge(setup_v, 1)
            pe.wait_ge(late_loaded, LATE)
            for m in range(PAIRS):
                for c in range(2):
                    last = pe.matmul(ps[0][:, m // 3, (m % 3) * REL:(m % 3 + 1) * REL], rk[:, c, m * P:(m + 1) * P],
                                     post[:, c, :], start=(c == 0), stop=(c == 1))
            last.then_inc(setup_mm, 1)
            pe.wait_ge(setup_v, 2)
            with pe.Fori(0, LARGE_STEPS) as n:
                step(n, False)
            pe.wait_ge(setup_p, 1)
            with pe.Fori(LARGE_STEPS, STEPS) as n:
                step(n, True)


def _chunked(w, rows):
    return w.reshape(-1, rows, w.shape[-1]).transpose(1, 0, 2)


def kernel(**inputs):
    import numpy as np
    import concourse.bacc as bacc
    from concourse.bass_utils import run_bass_kernel_spmd as run

    g = {k: np.asarray(v) for k, v in inputs.items()}
    side = g["x"].shape[-1] // 16
    patches = g["x"].reshape(IMAGES, 3, side, 16, side, 16).transpose(0, 2, 4, 3, 5, 1)
    columns = {"r_w": g["L0_attn_r_w_bias"], "r_r": g["L0_attn_r_r_bias"], "bk": g["L0_attn_bk"],
               "ln1_g": g["L0_tok_ln1_g"], "ln1_b": g["L0_tok_ln1_b"], "b_fc1": g["L0_ffn_b_fc1"]}
    vectors = {"tok_b": "L0_tok_b", "ln2_g": "L0_tok_ln2_g", "ln2_b": "L0_tok_ln2_b", "bv": "L0_attn_bv",
               "bo": "L0_attn_bo", "gamma": "L0_attn_gamma", "beta": "L0_attn_beta",
               "b_proj": "L0_ffn_b_proj", "b_fc2": "L0_ffn_b_fc2"}
    positions = g["L0_attn_position_embeds"][1:REL + 1].T
    w_qkv = g["L0_ffn_w_qkv"].reshape(D, 3, PAIRS // 2, 2, 2 * DV)
    w_qkv = np.concatenate([w_qkv[:, 0:2].transpose(0, 1, 3, 2, 4).reshape(D, 2 * D), w_qkv[:, 2].reshape(D, D)], axis=1)
    arrays = {
        "x": patches.reshape(STEPS, LANES, 2, TOK, PATCH),
        "w_tok": _chunked(g["L0_tok_W"].T, P),
        "w_q": g["L0_attn_Wq"], "w_k": g["L0_attn_Wk"], "w_v": g["L0_attn_Wv"],
        "r_kernel": _chunked(g["L0_attn_r_kernel"].reshape(D, PATCH), DC),
        "pos_t": _chunked(positions, DC),
        "w_o": _chunked(g["L0_attn_Wo"], DC),
        "w_qkv": _chunked(w_qkv, DC),
        "w_proj": _chunked(g["L0_ffn_w_proj"], DC),
        "w_fc1": _chunked(g["L0_ffn_w_fc1"], DC),
        "w_fc2": _chunked(g["L0_ffn_w_fc2"], P),
        "rows": np.stack([g[vectors[k]] for k in ROW_NAMES]),
        "cols6": np.stack([columns[k].reshape(6, P).T for k in COL6_NAMES], axis=1),
        "cols2": np.stack([g["L0_ffn_" + k].reshape(2, DC).T for k in COL2_NAMES], axis=1),
        "gumbel": g["L0_ffn_gumbel_weights"],
        "ident_in": np.eye(P, dtype=np.float32),
        "parity_in": np.tile(np.eye(2, dtype=np.float32).repeat(DV, axis=0), (DC // 32, 1)),
    }
    nc = bacc.Bacc("TRN2", target_bir_lowering=False, num_devices=1)
    feeds, args = {}, {}
    for name, a in arrays.items():
        a = np.ascontiguousarray(a)
        feeds[f"{name}_dram"] = a
        args[name] = nc.dram_tensor(f"{name}_dram", a.shape, mybir.dt.from_np(a.dtype), kind="ExternalInput").ap()
    args["out"] = nc.dram_tensor("out_dram", (STEPS, LANES, 2, TOK, D), F32, kind="ExternalOutput").ap()
    vit_tower(nc, **args)
    r = run(nc, [feeds], core_ids=[0])
    return r.results[0]["out_dram"].reshape(IMAGES, TOK, D)
```

```python
from contextlib import ExitStack

import concourse.bass as bass
from concourse import mybir
from concourse.alu_op_type import AluOpType as ALU

ACT = mybir.ActivationFunctionType
F32 = mybir.dt.float32
AX_X = mybir.AxisListType.X
AX_XY = mybir.AxisListType.XY

P = 128
TOK = 49
ROW = 64
ROWS = ROW + TOK
IMAGES = 16
LANES = 2
STEPS = IMAGES // 2 // LANES
LARGE_STEPS = STEPS // 2
D = 192
DC = 96
PATCH = 768
KC = PATCH // P
HEADS = 12
PAIRS = HEADS // 2
DH = 64
DV = D // HEADS
DV1 = DV + 1
REL = 2 * TOK - 1
RAW = HEADS * REL
SHIFTED = RAW - (TOK - 1)
HID = 4 * D
HC = HID // P
CHUNK = 3
EPS = 1e-5
EPS_ATTN = 1e-9
SCALE = DH ** -0.5
SCALE_FFN = DV ** -0.5
KEEP = (D, D // 2, D // 3)
ONES = DC
ATTN_LN = 3
FRONT_LN, BACK_LN = 3, 3

ROW_NAMES = ("tok_b", "ln2_g", "ln2_b", "bo", "gamma", "beta", "b_proj", "b_fc2")
COL6_NAMES = ("ln1_g", "ln1_b", "b_fc1")
COL2_NAMES = ("n1l_g", "n1l_b", "n1s_g", "n1s_b", "n2l_g", "n2l_b", "n2s_g", "n2s_b")


def vit_tower(nc, x, x_t, w_tok, w_q, w_qt, w_k, w_v, r_kernel, pos_t, w_o, w_qkv, w_proj, w_fc1, w_fc2,
              rows, cols6, cols2, gumbel, ident_in, out):
    with ExitStack() as ctx:
        def sb(name, shape):
            return ctx.enter_context(nc.sbuf_tensor(name, shape, F32))

        def sem(name):
            return ctx.enter_context(nc.semaphore(name))

        def lane_sb(name, shape):
            return [sb(f"{name}{w}", shape) for w in range(LANES)]

        def lane_sem(name):
            return [sem(f"{name}{w}") for w in range(LANES)]

        wtok = sb("wtok", [P, KC, D])
        wtok_mean = sb("wtok_mean", [P, D])
        wtok_c = sb("wtok_c", [P, KC, D])
        gain_768th = sb("gain_768th", [P, KC])
        wq = sb("wq", [DC + 1, 2, 384])
        wk = sb("wk", [DC + 1, 2, 384])
        wv = sb("wv", [DC + 1, 2, DC])
        wqt = sb("wqt", [P, PAIRS, DC + 1])
        rk = sb("rk", [DC, 2, PATCH])
        post = sb("post", [DC, 2, REL])
        rel = sb("rel", [P, PAIRS, REL])
        wrel = sb("wrel", [DC + 1, 2, PAIRS * REL])
        wo = sb("wo", [DC, 2, D])
        wqkv = sb("wqkv", [DC, 2, 3 * D])
        wproj = [sb("wproj_large", [DC, 2, D]), sb("wproj_small", [DC, 2, D])]
        w1 = sb("w1", [DC, 2, HID])
        w2 = sb("w2", [P, HC, D])
        w2_kept = [sb(f"w2_kept{v}", [P, HC, KEEP[v]]) for v in range(3)]
        row = sb("row", [P, len(ROW_NAMES), D])
        tok_bias = sb("tok_bias", [P, D])
        bproj_small = sb("bproj_small", [P, D])
        b2_small = sb("b2_small", [P, D])
        col6 = sb("col6", [P, len(COL6_NAMES), 6])
        col2 = sb("col2", [DC, len(COL2_NAMES), 2])
        gum = sb("gum", [P, 3])
        gum_sum = sb("gum_sum", [P, 3])
        ident = sb("ident", [P, P + 2])
        pool_eps = sb("pool_eps", [P, 2])
        minus_half = sb("minus_half", [P, 2])

        pool_zero = sb("pool_zero", [P, 1])
        table_in = sb("table_in", [P, 1])

        def c2(name):
            return col2[:, COL2_NAMES.index(name), :]

        def vec(name):
            return row[:, ROW_NAMES.index(name), :]

        def c6(name):
            return col6[:, COL6_NAMES.index(name), :]

        xt = lane_sb("xt", [P, PATCH])
        xT_first = lane_sb("xT_first", [P, KC, P])
        xT = lane_sb("xT", [P, KC, P])
        emb_mm = lane_sb("emb_mm", [P, D])
        emb = lane_sb("emb", [P, D])
        h = lane_sb("h", [P, D])
        qn = lane_sb("qn", [P, D])
        qn_bo = lane_sb("qn_bo", [P, D])
        h_beta = lane_sb("h_beta", [P, D])
        qnT = lane_sb("qnT", [DC + 1, 2, P])
        qw = lane_sb("qw", [P, PAIRS, P])
        k1 = lane_sb("k1", [P, PAIRS, P])
        v1 = lane_sb("v1", [P, 2, PAIRS, 2 * DV1])
        raw = lane_sb("raw", [P, RAW])
        posS = lane_sb("posS", [P, RAW])
        sc = lane_sb("sc", [P, HEADS * TOK])
        top = lane_sb("top", [P, HEADS])
        inv = lane_sb("inv", [P, HEADS])
        prob = lane_sb("prob", [P, PAIRS, 2, ROW])
        probT = lane_sb("probT", [P, PAIRS, P])
        av = lane_sb("av", [P, D])
        avT = lane_sb("avT", [DC, 2, P])
        y = lane_sb("y", [P, D])
        yc = lane_sb("yc", [P, D])
        h1 = lane_sb("h1", [P, D])
        f = lane_sb("f", [P, D])
        f_b = lane_sb("f_b", [P, D])
        nr = lane_sb("nr", [P, D])
        nT = lane_sb("nT", [DC, 2, P])
        q2 = lane_sb("q2", [DC, 2, P])
        k2 = lane_sb("k2", [DC, 2, 2, 2, TOK])
        v2 = lane_sb("v2", [P, 2, PAIRS, 2 * DV1])
        f2 = lane_sb("f2", [P, D])
        nr2 = lane_sb("nr2", [P, D])
        n2T = lane_sb("n2T", [DC, 2, P])
        hid = lane_sb("hid", [P, 6, CHUNK, P])
        rest = lane_sb("rest", [P, D])
        rest_b = lane_sb("rest_b", [P, D])
        res = lane_sb("res", [P, D])
        stats = lane_sb("stats", [P, 2, 6])
        mv = lane_sb("mv", [P, FRONT_LN + BACK_LN, 2])
        var_eps = lane_sb("var_eps", [P, 2])
        rstd = lane_sb("rstd", [P, FRONT_LN + BACK_LN, 2])
        scratch = [nc.dram_tensor(f"raw_scores{w}", [P, RAW], F32).ap() for w in range(LANES)]

        ps = [ctx.enter_context(nc.psum_tensor(f"ps{w}", [P, 4, 512], F32)) for w in range(LANES)]

        tok_loaded = sem("tok_loaded")
        early_loaded = sem("early_loaded")
        keys_loaded = sem("keys_loaded")
        rel_loaded = sem("rel_loaded")
        ffn_loaded = sem("ffn_loaded")
        xt_zeroed = sem("xt_zeroed")
        posS_zeroed = sem("posS_zeroed")
        zeroed_v = sem("zeroed_v")
        zeroed_p = sem("zeroed_p")
        zeroed_a = sem("zeroed_a")
        setup_mm = sem("setup_mm")
        bias_read = sem("bias_read")
        rel_mm = sem("rel_mm")
        rel_ready = sem("rel_ready")
        setup_v = sem("setup_v")
        setup_p = sem("setup_p")
        dve_chain = sem("dve_chain")
        pool_chain = sem("pool_chain")
        x_loaded = lane_sem("x_loaded")
        first_loaded = lane_sem("first_loaded")
        xT_loaded = lane_sem("xT_loaded")
        tok_mm = lane_sem("tok_mm")
        emb_ready = lane_sem("emb_ready")
        h_ready = lane_sem("h_ready")
        qn_ready = lane_sem("qn_ready")
        qnT_mm = lane_sem("qnT_mm")
        qnT_ready = lane_sem("qnT_ready")
        q_mm = lane_sem("q_mm")
        qw_ready = lane_sem("qw_ready")
        k_mm = lane_sem("k_mm")
        k_ready = lane_sem("k_ready")
        pos_mm = lane_sem("pos_mm")
        raw_ready = lane_sem("raw_ready")
        raw_stored = lane_sem("raw_stored")
        pos_loaded = lane_sem("pos_loaded")
        score_mm = [lane_sem("score_mm_a"), lane_sem("score_mm_b")]
        sc_ready = [lane_sem("sc_ready_a"), lane_sem("sc_ready_b")]
        prob_ready = [lane_sem("prob_ready_a"), lane_sem("prob_ready_b")]
        v_mm = [lane_sem("v_mm_a"), lane_sem("v_mm_b")]
        v_ready = [lane_sem("v_ready_a"), lane_sem("v_ready_b")]
        pT_mm = [lane_sem("pT_mm_a"), lane_sem("pT_mm_b")]
        pT_ready_act = [lane_sem("pT_act_a"), lane_sem("pT_act_b")]
        pT_ready_dve = [lane_sem("pT_dve_a"), lane_sem("pT_dve_b")]
        pv_mm = [lane_sem("pv_mm_a"), lane_sem("pv_mm_b")]
        av_ready = [lane_sem("av_ready_a"), lane_sem("av_ready_b")]
        avT_mm = [lane_sem("avT_mm_a"), lane_sem("avT_mm_b")]
        avT_ready = [lane_sem("avT_ready_a"), lane_sem("avT_ready_b")]
        o_mm = [lane_sem("o_mm_a"), lane_sem("o_mm_b")]
        front_var = lane_sem("front_var")
        front_rstd = lane_sem("front_rstd")
        back_var = lane_sem("back_var")
        back_rstd = lane_sem("back_rstd")
        qn_bo_ready = lane_sem("qn_bo_ready")
        h_beta_ready = lane_sem("h_beta_ready")
        h1_ready = lane_sem("h1_ready")
        f_ready = lane_sem("f_ready")
        f_b_ready = lane_sem("f_b_ready")
        nr_ready = lane_sem("nr_ready")
        nT_mm = lane_sem("nT_mm")
        nT_ready = lane_sem("nT_ready")
        q2_mm = lane_sem("q2_mm")
        q2_ready = lane_sem("q2_ready")
        k2_mm = lane_sem("k2_mm")
        k2_ready = lane_sem("k2_ready")
        f2_ready = lane_sem("f2_ready")
        nr2_ready = lane_sem("nr2_ready")
        n2T_mm = lane_sem("n2T_mm")
        n2T_ready = lane_sem("n2T_ready")
        fc1_mm = lane_sem("fc1_mm")
        gelu_ready = lane_sem("gelu_ready")
        fc2_mm = lane_sem("fc2_mm")
        rest_ready = lane_sem("rest_ready")
        res_ready = lane_sem("res_ready")
        res_free = lane_sem("res_free")

        BANKS = (1, 2)
        FRONT = 3
        TOK_LOADED = 16 * 2
        EARLY = 16 * 3
        KEYS_LOADED = 16 * 2
        REL_LOADED = 16 * 5
        FFN_LOADED = 16 * 5
        ZEROED_V = 2

        def chunks(small):
            return [(v, c) for v in range(3 if small else 1) for c in range(0, HC, CHUNK)]

        def chunk_count(n, j, small):
            large = len(chunks(False))
            if not small:
                return n * large + (j + 1)
            per = len(chunks(True))
            return n * per + (LARGE_STEPS * (large - per) + j + 1)

        def valid(ap):
            return ap.rearrange("p (b t) -> p b t", b=2)[:, :, 0:TOK]

        def turned(ap):
            return ap.rearrange("p (c t) -> p c t", t=P)[:, :, 0:ROWS]

        block = ctx.enter_context(nc.Block())

        @block.sync
        def _(sp):
            def load_x(m, w):
                for b in range(2):
                    sp.dma_start(xt[w][b * ROW:b * ROW + TOK, :], x[m, w, b]).then_inc(x_loaded[w], 16)

            def shift(m):
                for w in lanes:
                    sp.wait_ge(raw_ready[w], 4 * m + 4)
                    sp.dma_start(scratch[w][0:ROW + TOK, :], raw[w][0:ROW + TOK, :]).then_inc(raw_stored[w], 16)
                for w in lanes:
                    sp.wait_ge(raw_stored[w], 16 * m + 16)
                    for b in range(2):
                        skewed = bass.AP(scratch[w].tensor, b * ROW * RAW + TOK - 1, [[RAW - 1, TOK], [1, SHIFTED]])
                        sp.dma_start(posS[w][b * ROW:b * ROW + TOK, 0:SHIFTED], skewed).then_inc(pos_loaded[w], 16)

            def refill(m, w):
                sp.wait_ge(h_ready[w], m)
                sp.dma_start(xT[w][:], x_t[m, w]).then_inc(xT_loaded[w], 16)
                load_x(m, w)

            def store(n, w):
                sp.wait_ge(res_ready[w], n + 2)
                for b in range(2):
                    sp.dma_start(out[n, w, b], res[w][b * ROW:b * ROW + TOK, :]).then_inc(res_free[w], 16)

            lanes = range(LANES)
            for w in lanes:
                sp.dma_start(xT_first[w][:], x_t[0, w]).then_inc(first_loaded[w], 16)
            for w in lanes:
                sp.wait_ge(xt_zeroed, w + 1)
                load_x(0, w)
            for dst, src in ((wqt, w_qt), (wq, w_q), (wk, w_k), (wv, w_v), (wo, w_o)):
                sp.dma_start(dst[:], src).then_inc(rel_loaded, 16)
            for w in lanes:
                sp.dma_start(xT[w][:], x_t[1, w]).then_inc(xT_loaded[w], 16)
            for dst, src in ((col2, cols2), (wqkv, w_qkv), (wproj[0], w_proj), (w1, w_fc1), (w2, w_fc2)):
                sp.dma_start(dst[:], src).then_inc(ffn_loaded, 16)
            sp.wait_ge(posS_zeroed, LANES)
            for w in lanes:
                sp.wait_ge(front_var[w], 1)
                load_x(1, w)
            shift(0)
            with sp.Fori(0, LARGE_STEPS) as n:
                for w in lanes:
                    refill(n + 2, w)
                shift(n + 1)
                for w in lanes:
                    store(n, w)
            shift(STEPS - 1)
            for n in range(LARGE_STEPS, STEPS):
                for w in lanes:
                    store(n, w)
            for w in lanes:
                sp.wait_ge(res_free[w], 32 * STEPS + 32)

        @block.gpsimd
        def _(pool):
            chain = [0]

            def link(ins):
                chain[0] += 1
                ins.then_inc(pool_chain, 1)
                pool.wait_ge(pool_chain, chain[0])

            def restart():
                pool.sem_clear(pool_chain)
                chain[0] = 0

            for w in range(LANES):
                for values in (v1[w], v2[w]):
                    link(pool.memset(values[:], 0.0))
                    for r in range(2):
                        link(pool.memset(values[r * ROW:(r + 1) * ROW, :, :, r * DV1 + DV], 1.0))
                pool.memset(prob[w][:, :, :, TOK:ROW], 0.0)
                last = pool.memset(hid[w][:].rearrange("p j c (b t) -> p (j c b) t", b=2)[:, :, TOK:ROW], 0.0)
            last.then_inc(zeroed_p, 1)

            def moment(m, w, i):
                front = i < FRONT_LN
                var, done = (front_var, front_rstd) if front else (back_var, back_rstd)
                k = i if front else i - FRONT_LN
                pool.wait_ge(var[w], (FRONT_LN if front else BACK_LN) * m + (k + 1))
                return mv[w][:, i, 1:2], done[w]

            def rsqrt(m, w, i):
                var, done = moment(m, w, i)
                eps = pool_eps[:, 1:2] if i == ATTN_LN else pool_eps[:, 0:1]
                link(pool.tensor_tensor(var_eps[w][:, 0:1], var, eps, ALU.add))
                pool.tensor_tensor(rstd[w][:, i, 0:1], var_eps[w][:, 0:1], minus_half[:, 0:1],
                                   ALU.pow).then_inc(done, 1)

            def rsqrt_twice(m, w, i):
                var, done = moment(m, w, i)
                pool.tensor_tensor(var_eps[w][:, 0:1], var, pool_eps[:, 0:1], ALU.add)
                link(pool.tensor_scalar(var_eps[w][:, 1:2], var, 1.0 + EPS, EPS * EPS, ALU.mult, ALU.add))
                pool.tensor_tensor(rstd[w][:, i, :], var_eps[w][:], minus_half[:], ALU.pow).then_inc(done, 1)

            def front_patch(m):
                for w in lanes:
                    rsqrt(m, w, 0)

            def front_a(m):
                for i in (1, 2):
                    for w in lanes:
                        rsqrt(m, w, i)

            def front_b(m):
                for w in lanes:
                    pool.wait_ge(h_ready[w], m + 1)
                    pool.tensor_tensor(h_beta[w][:], h[w][:], vec("beta"), ALU.add).then_inc(h_beta_ready[w], 1)
                    pool.wait_ge(qn_ready[w], m + 1)
                    pool.tensor_tensor(qn_bo[w][:], qn[w][:], vec("bo"), ALU.add).then_inc(qn_bo_ready[w], 1)

            def step(n, small, ahead):
                restart()
                for w in lanes:
                    rsqrt(n, w, 3)
                for w in lanes:
                    rsqrt_twice(n, w, 4)
                for w in lanes:
                    pool.wait_ge(f_ready[w], n + 1)
                    pool.tensor_tensor(f_b[w][:], f[w][:], bproj_small[:] if small else vec("b_proj"),
                                       ALU.add).then_inc(f_b_ready[w], 1)
                if ahead:
                    front_b(n + 1)
                for w in lanes:
                    rsqrt(n, w, 5)
                if not small:
                    front_patch(n + 2)
                for w in lanes:
                    pool.wait_ge(f2_ready[w], n + 1)
                    link(pool.tensor_tensor(rest[w][:], h1[w][:], f2[w][:], ALU.add))
                    pool.tensor_tensor(rest_b[w][:], rest[w][:], b2_small[:] if small else vec("b_fc2"),
                                       ALU.add).then_inc(rest_ready[w], 1)
                if not small:
                    front_a(n + 2)

            def small_setup():
                restart()

                def times(dst, src, g):
                    link(pool.tensor_scalar(dst, src, g, 1.0, ALU.mult, ALU.mult))

                link(pool.tensor_tensor(gum_sum[:, 0:1], gum[:, 0:1], pool_zero[:], ALU.add))
                link(pool.tensor_tensor(gum_sum[:, 1:2], gum_sum[:, 0:1], gum[:, 1:2], ALU.add))
                link(pool.tensor_tensor(gum_sum[:, 2:3], gum_sum[:, 1:2], gum[:, 2:3], ALU.add))
                pool.wait_ge(ffn_loaded, FFN_LOADED)
                cuts = ((0, KEEP[2], 2), (KEEP[2], KEEP[1], 1), (KEEP[1], D, 0))
                for a, b, g in cuts:
                    times(bproj_small[:, a:b], vec("b_proj")[:, a:b], gum_sum[:, g:g + 1])
                    times(b2_small[:, a:b], vec("b_fc2")[:, a:b], gum_sum[:, g:g + 1])
                for a, b, g in cuts:
                    times(wproj[1][0:KEEP[2], 0, a:b], wproj[0][0:KEEP[2], 0, a:b], gum_sum[0:KEEP[2], g:g + 1])
                for a, b, g in ((0, KEEP[1], 1), (KEEP[1], D, 0)):
                    times(wproj[1][KEEP[2]:DC, 0, a:b], wproj[0][KEEP[2]:DC, 0, a:b], gum_sum[KEEP[2]:DC, g:g + 1])
                times(wproj[1][:, 1, :], wproj[0][:, 1, :], gum_sum[0:DC, 0:1])
                for v in range(2):
                    times(w2_kept[v][:], w2[:, :, 0:KEEP[v]], gum[:, v:v + 1])
                pool.tensor_scalar(w2_kept[2][:], w2[:, :, 0:KEEP[2]], gum[:, 2:3], 1.0, ALU.mult,
                                   ALU.mult).then_inc(setup_p, 1)

            lanes = range(LANES)
            pool.wait_ge(early_loaded, EARLY)
            pool.wait_ge(zeroed_v, ZEROED_V)
            restart()
            front_patch(0)
            front_a(0)
            front_b(0)
            front_patch(1)
            front_a(1)
            small_setup()
            with pool.Fori(0, LARGE_STEPS) as n:
                step(n, False, True)
            step(LARGE_STEPS, True, True)
            step(LARGE_STEPS + 1, True, False)

        @block.scalar
        def _(act):
            lanes = range(LANES)
            def zero_psum(w):
                act.activation(ps[w][:].rearrange("p b c -> p (b c)"), pool_zero[:].to_broadcast([P, 4 * 512]),
                               ACT.Copy).then_inc(zeroed_a, 1)

            for dst, src in ((wtok, w_tok), (col6, cols6)):
                act.dma_start(dst[:], src).then_inc(tok_loaded, 16)
            act.wait_ge(zeroed_v, 1)
            zero_psum(0)
            for dst, src in ((rk, r_kernel), (post, pos_t)):
                act.dma_start(dst[:], src).then_inc(keys_loaded, 16)
            for dst, src in ((row, bass.AP(rows.tensor, 0, [[0, P], [D, len(ROW_NAMES)], [1, D]])),
                             (ident, ident_in), (gum, bass.AP(gumbel.tensor, 0, [[0, P], [1, 3]]))):
                act.dma_start(dst[:], src).then_inc(early_loaded, 16)
            zero_psum(1)

            def transposed_probs(n, w, a):
                act.wait_ge(pT_mm[a][w], n + 1)
                act.activation(probT[w][:, 0:3, 0:ROWS], turned(ps[w][:, 0, 0:384]), ACT.Copy).then_inc(pT_ready_act[a][w], 1)

            def exp_scores(n, w, a):
                act.wait_ge(sc_ready[a][w], n + 1)
                if a == 0:
                    dst = prob[w][:, :, :, 0:TOK].rearrange("p m r t -> p r m t")
                    src = sc[w][:].rearrange("p (r m t) -> p r m t", r=2, t=TOK)
                else:
                    dst = prob[w][:, :, :, 0:TOK].rearrange("p m r t -> p (m r) t")
                    src = sc[w][:].rearrange("p (n t) -> p n t", t=TOK)
                act.activation(dst, src, ACT.Exp).then_inc(prob_ready[a][w], 1)

            def transposed_av(n, w, a):
                act.wait_ge(avT_mm[a][w], n + 1)
                act.activation(avT[w][:, :, 0:ROWS], turned(ps[w][0:DC, 1, 0:2 * P]), ACT.Copy).then_inc(avT_ready[a][w], 1)

            def affine_columns(n, w, done, dst, gain, shift, ready):
                act.wait_ge(done[w], n + 1)
                for c in range(2):
                    last = act.activation(dst[w][:, c, 0:ROWS], ps[w][0:DC, 1, c * P:c * P + ROWS], ACT.Identity,
                                          scale=gain[:, c:c + 1], bias=shift[:, c:c + 1])
                last.then_inc(ready[w], 1)

            def front_embed(m, bank=FRONT):
                for w in lanes:
                    act.wait_ge(tok_mm[w], m + 1)
                    act.activation(emb_mm[w][:], ps[w][:, bank, 0:D], ACT.Copy).then_inc(emb_ready[w], 1)

            def front_queries(m):
                for w in lanes:
                    act.wait_ge(qnT_mm[w], m + 1)
                    act.activation(qnT[w][0:DC, :, 0:ROWS], turned(ps[w][0:DC, FRONT, 0:2 * P]), ACT.Copy).then_inc(qnT_ready[w], 1)

            def raw_scores(m, g):
                for w in lanes:
                    act.wait_ge(pos_mm[w], 4 * m + (g + 1))
                    act.activation(raw[w][:, g * 3 * REL:(g + 1) * 3 * REL], ps[w][:, FRONT, 0:3 * REL],
                                   ACT.Copy).then_inc(raw_ready[w], 1)

            def step(n, small, ahead):
                size = "s" if small else "l"
                for w in lanes:
                    act.wait_ge(k_mm[w], n + 1)
                    for c in range(2):
                        last = act.activation(
                            k1[w][:, 3 * c:3 * c + 3, :].rearrange("p m (b t) -> p (m b) t", b=2)[:, :, 0:TOK],
                            ps[w][:, 2 + c, 0:6 * TOK].rearrange("p (q t) -> p q t", t=TOK), ACT.Copy)
                    last.then_inc(k_ready[w], 1)
                for w in lanes:
                    exp_scores(n, w, 0)
                if not small:
                    front_embed(n + 2)
                for w in lanes:
                    transposed_probs(n, w, 0)
                for w in lanes:
                    transposed_av(n, w, 0)
                if ahead:
                    front_queries(n + 1)
                    raw_scores(n + 1, 0)
                    raw_scores(n + 1, 1)
                    raw_scores(n + 1, 2)
                for w in lanes:
                    affine_columns(n, w, nT_mm, nT, c2(f"n1{size}_g"), c2(f"n1{size}_b"), nT_ready)
                for w in lanes:
                    exp_scores(n, w, 1)
                for w in lanes:
                    transposed_probs(n, w, 1)
                for w in lanes:
                    transposed_av(n, w, 1)
                act.activation(table_in[:], pool_zero[:], ACT.Gelu)
                if ahead:
                    raw_scores(n + 1, 3)
                for w in lanes:
                    affine_columns(n, w, n2T_mm, n2T, c2(f"n2{size}_g"), c2(f"n2{size}_b"), n2T_ready)
                for j, (v, c) in enumerate(chunks(small)):
                    for w in lanes:
                        act.wait_ge(fc1_mm[w], chunk_count(n, j, small))
                        for i in range(CHUNK):
                            last = act.activation(
                                valid(hid[w][:, j, i, :]),
                                ps[w][:, BANKS[j % 2], i * 2 * TOK:(i + 1) * 2 * TOK].rearrange("p (b t) -> p b t", b=2),
                                ACT.Gelu, bias=c6("b_fc1")[:, c + i:c + i + 1])
                        last.then_inc(gelu_ready[w], 1)

            act.wait_ge(rel_mm, 1)
            for r in range(2):
                last = act.activation(rel[:, 3 * r:3 * r + 3, :], ps[1][:, r, 0:3 * REL], ACT.Copy)
            last.then_inc(rel_ready, 1)
            front_embed(0)
            act.wait_ge(rel_mm, 2)
            for r in range(2):
                for c in range(2):
                    last = act.activation(wrel[:, c, :].rearrange("p (m r t) -> p m r t", r=2, t=REL)[:, :, r, :],
                                          ps[r][0:DC + 1, c, 0:3 * REL].rearrange("p (m t) -> p m t", t=REL),
                                          ACT.Copy, scale=SCALE)
            last.then_inc(rel_ready, 1)
            front_queries(0)
            front_embed(1, bank=2)
            for g in range(4):
                raw_scores(0, g)
            act.wait_ge(ffn_loaded, FFN_LOADED)
            act.wait_ge(zeroed_p, 1)
            with act.Fori(0, LARGE_STEPS) as n:
                step(n, False, True)
            step(LARGE_STEPS, True, True)
            step(LARGE_STEPS + 1, True, False)

        @block.vector
        def _(dve):
            lanes = range(LANES)
            chain = [0]

            def link(ins):
                chain[0] += 1
                ins.then_inc(dve_chain, 1)
                dve.wait_ge(dve_chain, chain[0])

            def restart():
                dve.sem_clear(dve_chain)
                chain[0] = 0

            dve.memset(pool_zero[:], 0.0).then_inc(zeroed_v, 1)
            for w in lanes:
                dve.memset(xt[w][:], 0.0).then_inc(xt_zeroed, 1)
            dve.memset(pool_eps[:, 0:1], EPS)
            dve.memset(pool_eps[:, 1:2], EPS_ATTN)
            dve.memset(minus_half[:], -0.5).then_inc(zeroed_v, 1)
            dve.wait_ge(tok_loaded, TOK_LOADED)
            dve.tensor_scalar(gain_768th[:], c6("ln1_g"), 1.0 / PATCH, None, ALU.mult).then_inc(setup_v, 1)
            for w in lanes:
                dve.memset(res[w][:, 0:DC], 0.0).then_inc(res_free[w], 32)
                dve.memset(res[w][:, DC:D], 0.0).then_inc(res_ready[w], 1)
                dve.memset(posS[w][:], 0.0).then_inc(posS_zeroed, 1)
                dve.memset(qnT[w][ONES:ONES + 1], 1.0)
                dve.memset(inv[w][:], 1.0)

            def fold():
                dve.wait_ge(setup_mm, 1)
                link(dve.tensor_copy(wtok_mean[:], ps[0][:, 0, 0:D]))
                for c in range(KC):
                    last = dve.scalar_tensor_tensor(out=wtok_c[:, c, :], in0=wtok[:, c, :], scalar=c6("ln1_g")[:, c:c + 1],
                                                    in1=wtok_mean[:], op0=ALU.mult, op1=ALU.subtract)
                last.then_inc(setup_v, 1)
                dve.wait_ge(setup_mm, 2)
                dve.wait_ge(early_loaded, EARLY)
                dve.tensor_tensor(tok_bias[:], ps[0][:, 1, 0:D], vec("tok_b"), ALU.add).then_inc(bias_read, 1)
                dve.wait_ge(bias_read, 1)

            def moments(w, i, src):
                k = src.shape[1] // 384 or 1
                size = src.shape[1] // k
                for j in range(k):
                    last = dve.bn_stats(stats[w][:, j, :], src[:, j * size:(j + 1) * size])
                link(last)
                var = (front_var if i < FRONT_LN else back_var)[w]
                dve.bn_aggr(mv[w][:, i, :], stats[w][:, 0:k, :]).then_inc(var, 1)

            def mean(w, i):
                return mv[w][:, i, 0:1]

            def inv_dev(w, i, twice=0):
                return rstd[w][:, i, twice:twice + 1]

            def rstd_done(m, w, i):
                if i < FRONT_LN:
                    dve.wait_ge(front_rstd[w], m * FRONT_LN + (i + 1))
                else:
                    dve.wait_ge(back_rstd[w], m * BACK_LN + (i - FRONT_LN + 1))

            def normalise(m, w, i, src, dst, twice=0):
                rstd_done(m, w, i)
                return dve.tensor_scalar(dst, src, mean(w, i), inv_dev(w, i, twice), ALU.subtract, ALU.mult)

            def normalise_affine(m, w, i, src, gain, shift, dst):
                centre(w, i, src, gain)
                return scale_shift(m, w, i, shift, dst)

            def centre(w, i, src, gain):
                link(dve.scalar_tensor_tensor(out=yc[w][:], in0=src, scalar=mean(w, i), in1=gain,
                                              op0=ALU.subtract, op1=ALU.mult))

            def scale_shift(m, w, i, shift, dst):
                rstd_done(m, w, i)
                return dve.scalar_tensor_tensor(out=dst, in0=yc[w][:], scalar=inv_dev(w, i), in1=shift,
                                                op0=ALU.mult, op1=ALU.add)

            def per_head(ap):
                return ap.unsqueeze(2).to_broadcast([P, HEADS, TOK])

            def softmax_front(n, w, a):
                flat = sc[w][:].rearrange("p (n t) -> p n t", t=TOK)
                if a == 0:
                    dve.wait_ge(pos_loaded[w], 32 * n + 32)
                    dve.wait_ge(score_mm[0][w], n + 1)
                    link(dve.tensor_tensor(
                        sc[w][:].rearrange("p (r m t) -> p r m t", r=2, t=TOK),
                        ps[w][:, 1:3, 0:PAIRS * TOK].rearrange("p r (m t) -> p r m t", t=TOK),
                        posS[w][:].rearrange("p (m r t) -> p r m t", r=2, t=REL)[:, :, :, 0:TOK], ALU.add))
                    src, top_src = flat, flat
                    top_dst = top[w][:]
                else:
                    dve.wait_ge(score_mm[1][w], n + 1)
                    src = ps[w][:, 0:3, 0:4 * TOK].rearrange("p g (q t) -> p g q t", t=TOK)
                    top_src, top_dst = src, top[w][:].rearrange("p (g q) -> p g q", g=3)
                link(dve.tensor_reduce(top_dst, top_src, AX_X, ALU.max))
                if a == 0:
                    last = dve.tensor_tensor(flat, flat, per_head(top[w][:]), ALU.subtract)
                else:
                    last = dve.tensor_tensor(
                        sc[w][:].rearrange("p (g q t) -> p g q t", g=3, t=TOK), src,
                        top[w][:].rearrange("p (g q) -> p g q", g=3).unsqueeze(3).to_broadcast([P, 3, 4, TOK]),
                        ALU.subtract)
                last.then_inc(sc_ready[a][w], 1)

            def values(n, w, a):
                dst = (v1, v2)[a][w]
                dve.wait_ge(v_mm[a][w], n + 1)
                for r in range(2):
                    rows_ = slice(r * ROW, (r + 1) * ROW)
                    o = dst[rows_, :, :, r * DV1:r * DV1 + DV]
                    i = ps[w][rows_, 0, 0:D].rearrange("p (b m d) -> p b m d", b=2, d=DV)
                    last = dve.tensor_copy(o, i)
                last.then_inc(v_ready[a][w], 1)

            def transposed_probs(n, w, a):
                dve.wait_ge(pT_mm[a][w], n + 1)
                dve.tensor_copy(probT[w][:, 3:6, 0:ROWS], turned(ps[w][:, 1, 0:384])).then_inc(
                    pT_ready_dve[a][w], 1)

            def attended(n, w, a):
                dve.wait_ge(pv_mm[a][w], n + 1)
                sums = ps[w][:, 2, 0:HEADS * DV1].rearrange("p (n d) -> p n d", d=DV1)
                for b in range(2):
                    toks = slice(b * ROW, b * ROW + TOK)
                    last = dve.reciprocal(inv[w][toks, :], sums[toks, :, DV])
                link(last)
                dve.tensor_tensor(av[w][:].rearrange("p (n d) -> p n d", d=DV), sums[:, :, 0:DV],
                                  inv[w][:].unsqueeze(2).to_broadcast([P, HEADS, DV]),
                                  ALU.mult).then_inc(av_ready[a][w], 1)

            def front_patch(m):
                for w in lanes:
                    dve.wait_ge(x_loaded[w], 32 * m + 32)
                    moments(w, 0, xt[w][:])

            def front_embed(m):
                for w in lanes:
                    dve.wait_ge(emb_ready[w], m + 1)
                    rstd_done(m, w, 0)
                    link(dve.scalar_tensor_tensor(out=emb[w][:], in0=emb_mm[w][:], scalar=inv_dev(w, 0),
                                                  in1=tok_bias[:], op0=ALU.mult, op1=ALU.add))
                    moments(w, 1, emb[w][:])

            def front_h(m, first=False):
                for w in lanes:
                    if not first:
                        dve.wait_ge(h_beta_ready[w], m)
                    normalise_affine(m, w, 1, emb[w][:], vec("ln2_g"), vec("ln2_b"), h[w][:]).then_inc(h_ready[w], 1)
                    dve.wait_ge(h_ready[w], m + 1)
                    moments(w, 2, h[w][:])

            def front_query(m, first=False):
                for w in lanes:
                    if not first:
                        dve.wait_ge(qn_bo_ready[w], m)
                        dve.wait_ge(qnT_mm[w], m)
                    normalise(m, w, 2, h[w][:], qn[w][:]).then_inc(qn_ready[w], 1)

            def step(n, small, ahead):
                restart()
                for w in lanes:
                    dve.wait_ge(q_mm[w], n + 1)
                    for c in range(2):
                        last = dve.tensor_scalar(
                            qw[w][:, 3 * c:3 * c + 3, :].rearrange("p m (b t) -> p (m b) t", b=2)[:, :, 0:TOK],
                            ps[w][:, c, 0:6 * TOK].rearrange("p (q t) -> p q t", t=TOK), SCALE, None, ALU.mult)
                    last.then_inc(qw_ready[w], 1)
                for w in lanes:
                    values(n, w, 0)
                    softmax_front(n, w, 0)
                for w in lanes:
                    transposed_probs(n, w, 0)
                for w in lanes:
                    attended(n, w, 0)
                for w in lanes:
                    dve.wait_ge(qn_bo_ready[w], n + 1)
                    dve.wait_ge(o_mm[0][w], n + 1)
                    link(dve.tensor_tensor(y[w][:], ps[w][:, 0, 0:D], qn_bo[w][:], ALU.add))
                    moments(w, 3, y[w][:])
                for w in lanes:
                    dve.wait_ge(h_beta_ready[w], n + 1)
                    normalise_affine(n, w, 3, y[w][:], vec("gamma"), h_beta[w][:], h1[w][:]).then_inc(h1_ready[w], 1)
                    dve.wait_ge(h1_ready[w], n + 1)
                    moments(w, 4, h1[w][:])
                for w in lanes:
                    normalise(n, w, 4, h1[w][:], nr[w][:], twice=1).then_inc(nr_ready[w], 1)
                    normalise(n, w, 4, h1[w][:], f[w][:]).then_inc(f_ready[w], 1)
                for w in lanes:
                    dve.wait_ge(q2_mm[w], n + 1)
                    dve.tensor_scalar(q2[w][:].rearrange("p c (b t) -> p c b t", b=2)[:, :, :, 0:TOK],
                                      ps[w][0:DC, 2, 0:4 * TOK].rearrange("p (c b t) -> p c b t", c=2, b=2),
                                      SCALE_FFN, None, ALU.mult).then_inc(q2_ready[w], 1)
                    dve.wait_ge(k2_mm[w], n + 1)
                    for r in range(2):
                        last = dve.tensor_scalar(k2[w][:, :, :, r, :],
                                                 ps[w][0:DC, 1, 0:4 * TOK].rearrange("p (c b t) -> p c b t", c=2, b=2),
                                                 ident[0:DC, P + r:P + r + 1], None, ALU.mult)
                    last.then_inc(k2_ready[w], 1)
                    values(n, w, 1)
                for w in lanes:
                    softmax_front(n, w, 1)
                for w in lanes:
                    transposed_probs(n, w, 1)
                for w in lanes:
                    attended(n, w, 1)
                for w in lanes:
                    dve.wait_ge(f_b_ready[w], n + 1)
                    dve.wait_ge(o_mm[1][w], n + 1)
                    dve.tensor_tensor(f2[w][:], ps[w][:, 0, 0:D], f_b[w][:], ALU.add).then_inc(f2_ready[w], 1)
                    dve.wait_ge(f2_ready[w], n + 1)
                    moments(w, 5, f2[w][:])
                for w in lanes:
                    normalise(n, w, 5, f2[w][:], nr2[w][:]).then_inc(nr2_ready[w], 1)
                if not small:
                    front_patch(n + 2)
                    front_embed(n + 2)
                    front_h(n + 2)
                    front_query(n + 2)
                for w in lanes:
                    dve.wait_ge(rest_ready[w], n + 1)
                    dve.wait_ge(res_free[w], 32 * n + 32)
                    dve.wait_ge(fc2_mm[w], n + 1)
                    dve.tensor_tensor(res[w][:], ps[w][:, 0, 0:D], rest_b[w][:], ALU.add).then_inc(res_ready[w], 1)

            fold()
            restart()
            front_patch(0)
            front_embed(0)
            front_h(0, first=True)
            front_query(0, first=True)
            front_patch(1)
            front_embed(1)
            front_h(1)
            front_query(1)
            with dve.Fori(0, LARGE_STEPS) as n:
                step(n, False, True)
            step(LARGE_STEPS, True, True)
            step(LARGE_STEPS + 1, True, False)

        @block.tensor
        def _(pe):
            lanes = range(LANES)

            def features(src, w):
                def into(bank):
                    for c in range(2):
                        last = pe.transpose(ps[w][0:DC, bank, c * P:c * P + ROWS], src[w][0:ROWS, c * DC:(c + 1) * DC],
                                            ident[0:ROWS, 0:ROWS])
                    return last
                return into

            def every_other(weights, r):
                return weights.rearrange("p (m r d) -> p m r d", r=2, d=DV)[:, :, r, :]

            def tokens(srcT, w, c):
                return valid(srcT[w][:, c, :])

            def back(n, w, a, weights):
                vals = (v1, v2)[a][w]

                def transposes():
                    pe.wait_ge(prob_ready[a][w], n + 1)
                    pe.wait_ge(v_ready[a][w], n + 1)
                    for m in range(PAIRS):
                        last = pe.transpose(ps[w][:, m // 3, (m % 3) * P:(m % 3) * P + ROWS],
                                            prob[w][0:ROWS, m, :, :].rearrange("p r t -> p (r t)"),
                                            ident[0:ROWS, 0:ROWS])
                    last.then_inc(pT_mm[a][w], 1)

                def attend():
                    pe.wait_ge(pT_ready_act[a][w], n + 1)
                    pe.wait_ge(pT_ready_dve[a][w], n + 1)
                    for b in range(2):
                        for m in range(PAIRS):
                            last = pe.matmul(ps[w][b * ROW:b * ROW + TOK, 2, m * 2 * DV1:(m + 1) * 2 * DV1],
                                             probT[w][:, m, b * ROW:b * ROW + TOK], vals[:, b, m, :],
                                             start=True, stop=True)
                    last.then_inc(pv_mm[a][w], 1)

                def turn():
                    pe.wait_ge(av_ready[a][w], n + 1)
                    features(av, w)(1).then_inc(avT_mm[a][w], 1)

                def project():
                    pe.wait_ge(avT_ready[a][w], n + 1)
                    for c in range(2):
                        last = pe.matmul(ps[w][0:ROWS, 0, 0:D], avT[w][:, c, 0:ROWS], weights[:, c, :],
                                         start=(c == 0), stop=(c == 1))
                    last.then_inc(o_mm[a][w], 1)

                return transposes, attend, turn, project

            def front_embed(src, loaded, count, bank):
                for w in lanes:
                    pe.wait_ge(loaded[w], count)
                    for c in range(KC):
                        last = pe.matmul(ps[w][:, bank, 0:D], src[w][:, c, :], wtok_c[:, c, :],
                                         start=(c == 0), stop=(c == KC - 1))
                    last.then_inc(tok_mm[w], 1)

            def front_queries(m):
                for w in lanes:
                    pe.wait_ge(qn_ready[w], m + 1)
                    features(qn, w)(FRONT).then_inc(qnT_mm[w], 1)

            def all_read(read, count):
                for w in lanes:
                    pe.wait_ge(read[w], count)

            def front_scores(m, g):
                for w in lanes:
                    if g == 0:
                        pe.wait_ge(qnT_ready[w], m + 1)
                    else:
                        pe.wait_ge(raw_ready[w], 4 * m + g)
                    pe.matmul(ps[w][0:ROWS, FRONT, 0:3 * REL], qnT[w][:, g // 2, 0:ROWS],
                              wrel[:, g // 2, (g % 2) * 3 * REL:(g % 2 + 1) * 3 * REL],
                              start=True, stop=True).then_inc(pos_mm[w], 1)

            def fc1(n, w, j, v, c, small):
                if j == 0:
                    pe.wait_ge(n2T_ready[w], n + 1)
                if j >= 2:
                    pe.wait_ge(gelu_ready[w], chunk_count(n, j - 2, small))
                keep = KEEP[v]
                for i in range(CHUNK):
                    dst = ps[w][:, BANKS[j % 2], i * 2 * TOK:(i + 1) * 2 * TOK]
                    cols = slice((c + i) * P, (c + i + 1) * P)
                    for kc in range(2 if keep > DC else 1):
                        k = min(keep, DC)
                        last = pe.matmul(dst, w1[0:k, kc, cols], valid(n2T[w][0:k, kc, :]),
                                         start=(kc == 0), stop=(kc == 1 or keep <= DC))
                last.then_inc(fc1_mm[w], 1)

            def fc2(n, w, j, v, c, small):
                pe.wait_ge(gelu_ready[w], chunk_count(n, j, small))
                weights = w2_kept[v] if small else w2
                for i in range(CHUNK):
                    first = j == 0 and i == 0
                    final = j == len(chunks(small)) - 1 and i == CHUNK - 1
                    last = pe.matmul(ps[w][:, 0, 0:KEEP[v]], hid[w][:, j, i, :], weights[:, c + i, :],
                                     start=first, stop=final, skip_group_check=True)
                if final:
                    last.then_inc(fc2_mm[w], 1)

            def step(n, small, ahead):
                for w in lanes:
                    pe.wait_ge(raw_ready[w], 4 * n + 4)
                    pe.wait_ge(res_ready[w], n + 1)
                    for bank, weights, done in ((0, wq, q_mm), (2, wk, k_mm)):
                        for m in range(PAIRS):
                            o = (m % 3) * 2 * TOK
                            last = pe.matmul(ps[w][:, bank + m // 3, o:o + 2 * TOK],
                                             weights[:, m // 3, (m % 3) * P:(m % 3 + 1) * P],
                                             tokens(qnT, w, m // 3), start=True, stop=True)
                        last.then_inc(done[w], 1)
                for w in lanes:
                    pe.wait_ge(k_ready[w], n + 1)
                    pe.wait_ge(qw_ready[w], n + 1)
                    for b in range(2):
                        for r in range(2):
                            for c in range(2):
                                last = pe.matmul(ps[w][r * ROW:r * ROW + TOK, 0, b * DC + c * 48:b * DC + (c + 1) * 48],
                                                 qnT[w][:, c, b * ROW:b * ROW + TOK], every_other(wv[:, c, :], r),
                                                 start=True, stop=True)
                    last.then_inc(v_mm[0][w], 1)
                    for m in range(PAIRS):
                        for b in range(2):
                            cols = slice(b * ROW, b * ROW + TOK)
                            for r in range(2):
                                half = slice(r * DH, (r + 1) * DH)
                                last = pe.matmul(ps[w][b * ROW:b * ROW + TOK, 1 + r, m * TOK:(m + 1) * TOK],
                                                 qw[w][half, m, cols], k1[w][half, m, cols], start=True, stop=True)
                    last.then_inc(score_mm[0][w], 1)
                if not small:
                    front_embed(xT, xT_loaded, 16 * n + 32, FRONT)
                first = [back(n, w, 0, wo) for w in lanes]
                for stage in range(4):
                    for w in lanes:
                        first[w][stage]()
                if ahead:
                    if not small:
                        all_read(emb_ready, n + 3)
                    front_queries(n + 1)
                    front_scores(n + 1, 0)
                    front_scores(n + 1, 1)
                    front_scores(n + 1, 2)
                for w in lanes:
                    pe.wait_ge(nr_ready[w], n + 1)
                    features(nr, w)(1).then_inc(nT_mm[w], 1)
                for w in lanes:
                    pe.wait_ge(nT_ready[w], n + 1)
                    for bank, first, done in ((2, 0, q2_mm), (1, D, k2_mm)):
                        for c in range(2):
                            for kc in range(2):
                                cols = wqkv[:, kc, first + c * DC:first + (c + 1) * DC]
                                last = pe.matmul(ps[w][0:DC, bank, c * 2 * TOK:(c + 1) * 2 * TOK], cols,
                                                 tokens(nT, w, kc), start=(kc == 0), stop=(kc == 1))
                        last.then_inc(done[w], 1)
                    for b in range(2):
                        for r in range(2):
                            for c in range(2):
                                last = pe.matmul(ps[w][r * ROW:r * ROW + TOK, 0, b * DC:(b + 1) * DC],
                                                 nT[w][:, c, b * ROW:b * ROW + TOK],
                                                 every_other(wqkv[:, c, 2 * D:3 * D], r),
                                                 start=(c == 0), stop=(c == 1))
                    last.then_inc(v_mm[1][w], 1)
                for w in lanes:
                    pe.wait_ge(q2_ready[w], n + 1)
                    pe.wait_ge(k2_ready[w], n + 1)
                    pe.wait_ge(v_ready[1][w], n + 1)
                    for c in range(2):
                        for b in range(2):
                            for g in range(3):
                                part = slice(g * 32, (g + 1) * 32)
                                last = pe.matmul(ps[w][b * ROW:b * ROW + TOK, g, c * 2 * TOK:(c + 1) * 2 * TOK],
                                                 q2[w][part, c, b * ROW:b * ROW + TOK],
                                                 k2[w][part, c, b, :, :].rearrange("p r t -> p (r t)"),
                                                 start=True, stop=True)
                    last.then_inc(score_mm[1][w], 1)
                second = [back(n, w, 1, wproj[small]) for w in lanes]
                for stage in range(4):
                    for w in lanes:
                        second[w][stage]()
                if ahead:
                    front_scores(n + 1, 3)
                for w in lanes:
                    pe.wait_ge(nr2_ready[w], n + 1)
                    features(nr2, w)(1).then_inc(n2T_mm[w], 1)
                todo = chunks(small)
                for j in range(len(todo) + 2):
                    for w in lanes:
                        if j < len(todo):
                            fc1(n, w, j, *todo[j], small)
                        if j >= 2:
                            fc2(n, w, j - 2, *todo[j - 2], small)

            pe.wait_ge(zeroed_a, 1)
            pe.wait_ge(tok_loaded, TOK_LOADED)
            pe.wait_ge(setup_v, 1)
            for bank, lhs in ((0, gain_768th), (1, c6("ln1_b"))):
                for c in range(KC):
                    last = pe.matmul(ps[0][:, bank, 0:D], lhs[:, c:c + 1].to_broadcast([P, P]), wtok[:, c, :],
                                     start=(c == 0), stop=(c == KC - 1))
                last.then_inc(setup_mm, 1)
            pe.wait_ge(zeroed_a, 2)
            pe.wait_ge(keys_loaded, KEYS_LOADED)
            for m in range(PAIRS):
                for c in range(2):
                    last = pe.matmul(ps[1][:, m // 3, (m % 3) * REL:(m % 3 + 1) * REL], rk[:, c, m * P:(m + 1) * P],
                                     post[:, c, :], start=(c == 0), stop=(c == 1))
            last.then_inc(rel_mm, 1)
            pe.wait_ge(setup_v, 2)
            front_embed(xT_first, first_loaded, 16, FRONT)
            pe.wait_ge(rel_loaded, REL_LOADED)
            pe.wait_ge(rel_ready, 1)
            pe.wait_ge(bias_read, 1)
            for m in range(PAIRS):
                for r in range(2):
                    half = slice(r * DH, (r + 1) * DH)
                    last = pe.matmul(ps[r][0:DC + 1, m // 3, (m % 3) * REL:(m % 3 + 1) * REL], wqt[half, m, :],
                                     rel[half, m, :], start=True, stop=True)
            last.then_inc(rel_mm, 1)
            front_embed(xT, xT_loaded, 16, 2)
            pe.wait_ge(rel_ready, 2)
            pe.wait_ge(early_loaded, EARLY)
            pe.wait_ge(zeroed_p, 1)
            all_read(emb_ready, 1)
            front_queries(0)
            for g in range(4):
                front_scores(0, g)
            all_read(emb_ready, 2)
            pe.wait_ge(ffn_loaded, FFN_LOADED)
            with pe.Fori(0, LARGE_STEPS) as n:
                step(n, False, True)
            pe.wait_ge(setup_p, 1)
            step(LARGE_STEPS, True, True)
            step(LARGE_STEPS + 1, True, False)


def _chunked(w, rows):
    return w.reshape(-1, rows, w.shape[-1]).transpose(1, 0, 2)


def kernel(**inputs):
    import numpy as np
    import concourse.bacc as bacc
    from concourse.bass_utils import run_bass_kernel_spmd as run

    g = {k: np.asarray(v) for k, v in inputs.items()}
    side = g["x"].shape[-1] // 16
    patches = g["x"].reshape(IMAGES, 3, side, 16, side, 16).transpose(0, 2, 4, 3, 5, 1)
    patches = patches.reshape(STEPS, LANES, 2, TOK, KC, P)
    patches_t = np.zeros((STEPS, LANES, P, KC, 2, ROW), np.float32)
    patches_t[..., 0:TOK] = patches.transpose(0, 1, 5, 4, 2, 3)
    w_qt = np.zeros((HEADS, DH, DC + 1), np.float32)
    for n in range(HEADS):
        group, at = n // 3, (n // 3 % 2) * 48
        w_qt[n, :, at:at + 48] = g["L0_attn_Wq"][group][:, (n % 3) * DH:(n % 3 + 1) * DH].T
        w_qt[n, :, ONES] = g["L0_attn_r_r_bias"][n]
    def grouped(weights, bias):
        w = np.zeros((DC + 1, 2, 2 * weights.shape[-1]), np.float32)
        for k in range(4):
            r, c = k % 2 * 48, k % 2 * weights.shape[-1]
            w[r:r + 48, k // 2, c:c + weights.shape[-1]] = weights[k]
        w[ONES] = bias.reshape(2, -1)
        return w

    parity = np.zeros((P, 2), np.float32)
    for r in range(2):
        parity.reshape(P // 32, 2, DV, 2)[:, r, :, r] = 1.0
    columns = {"ln1_g": g["L0_tok_ln1_g"], "ln1_b": g["L0_tok_ln1_b"], "b_fc1": g["L0_ffn_b_fc1"]}
    vectors = {"tok_b": "L0_tok_b", "ln2_g": "L0_tok_ln2_g", "ln2_b": "L0_tok_ln2_b", 
               "bo": "L0_attn_bo", "gamma": "L0_attn_gamma", "beta": "L0_attn_beta",
               "b_proj": "L0_ffn_b_proj", "b_fc2": "L0_ffn_b_fc2"}
    positions = g["L0_attn_position_embeds"][1:REL + 1].T
    w_qkv = g["L0_ffn_w_qkv"].reshape(D, 3, PAIRS // 2, 2, 2 * DV)
    w_qkv = np.concatenate([w_qkv[:, 0:2].transpose(0, 1, 3, 2, 4).reshape(D, 2 * D), w_qkv[:, 2].reshape(D, D)], axis=1)
    arrays = {
        "x": patches.reshape(STEPS, LANES, 2, TOK, PATCH),
        "x_t": patches_t.reshape(STEPS, LANES, P, KC, P),
        "w_qt": w_qt.reshape(PAIRS, P, DC + 1).transpose(1, 0, 2),
        "w_tok": _chunked(g["L0_tok_W"].T, P),
        "w_q": grouped(g["L0_attn_Wq"], g["L0_attn_r_w_bias"]),
        "w_k": grouped(g["L0_attn_Wk"], g["L0_attn_bk"]),
        "w_v": grouped(g["L0_attn_Wv"], g["L0_attn_bv"]),
        "r_kernel": _chunked(g["L0_attn_r_kernel"].reshape(D, PATCH), DC),
        "pos_t": _chunked(positions, DC),
        "w_o": _chunked(g["L0_attn_Wo"], DC),
        "w_qkv": _chunked(w_qkv, DC),
        "w_proj": _chunked(g["L0_ffn_w_proj"], DC),
        "w_fc1": _chunked(g["L0_ffn_w_fc1"], DC),
        "w_fc2": _chunked(g["L0_ffn_w_fc2"], P),
        "rows": np.stack([g[vectors[k]] for k in ROW_NAMES]),
        "cols6": np.stack([columns[k].reshape(6, P).T for k in COL6_NAMES], axis=1),
        "cols2": np.stack([g["L0_ffn_" + k].reshape(2, DC).T for k in COL2_NAMES], axis=1),
        "gumbel": g["L0_ffn_gumbel_weights"],
        "ident_in": np.concatenate([np.eye(P, dtype=np.float32), parity], axis=1),
    }
    nc = bacc.Bacc("TRN2", target_bir_lowering=False, num_devices=1)
    feeds, args = {}, {}
    for name, a in arrays.items():
        a = np.ascontiguousarray(a)
        feeds[f"{name}_dram"] = a
        args[name] = nc.dram_tensor(f"{name}_dram", a.shape, mybir.dt.from_np(a.dtype), kind="ExternalInput").ap()
    args["out"] = nc.dram_tensor("out_dram", (STEPS, LANES, 2, TOK, D), F32, kind="ExternalOutput").ap()
    vit_tower(nc, **args)
    r = run(nc, [feeds], core_ids=[0])
    return r.results[0]["out_dram"].reshape(IMAGES, TOK, D)
```

```python
from contextlib import ExitStack

import concourse.bass as bass
from concourse import mybir
from concourse.alu_op_type import AluOpType as ALU

ACT = mybir.ActivationFunctionType
F32 = mybir.dt.float32
AX_X = mybir.AxisListType.X

P = 128
TOK = 49
ROW = 64
ROWS = ROW + TOK
IMAGES = 16
LANES = 2
STEPS = IMAGES // 2 // LANES
LARGE_STEPS = STEPS // 2
D = 192
DC = 96
PATCH = 768
KC = PATCH // P
HEADS = 12
PAIRS = HEADS // 2
DH = 64
DV = D // HEADS
DV1 = DV + 1
REL = 2 * TOK - 1
RAW = HEADS * REL
SHIFTED = RAW - (TOK - 1)
HID = 4 * D
HC = HID // P
CHUNK = 2
GROUPS = HC // CHUNK
EPS = 1e-5
EPS_ATTN = 1e-9
SCALE = DH ** -0.5
SCALE_FFN = DV ** -0.5
KEEP = (D, D // 2, D // 3)
FEAT = D // 4
WIDE = ROW + FEAT + 1
ATTN_LN = 3
FRONT_LN, BACK_LN = 3, 3

ROW_NAMES = ("tok_b", "ln2_g", "ln2_b", "bo", "gamma", "beta", "b_proj", "b_fc2")
COL6_NAMES = ("ln1_g", "ln1_b", "b_fc1")
COL2_NAMES = ("n1l_g", "n1l_b", "n1s_g", "n1s_b", "n2l_g", "n2l_b", "n2s_g", "n2s_b")


def vit_tower(nc, x, x_t, w_tok, w_qc, w_qt, w_kt, w_v, r_kernel, pos_t, w_o, w_qkv, w_proj, w_fc1, w_fc2,
              rows, cols6, cols2, gumbel, ident_in, out):
    with ExitStack() as ctx:
        def sb(name, shape):
            return ctx.enter_context(nc.sbuf_tensor(name, shape, F32))

        def sem(name):
            return ctx.enter_context(nc.semaphore(name))

        def lane_sb(name, shape):
            return [sb(f"{name}{w}", shape) for w in range(LANES)]

        def shared_sb(name, shape):
            whole = sb(name, [*shape[:-1], LANES * shape[-1]])
            tail = (slice(None),) * (len(shape) - 1)
            return whole, [whole[tail + (slice(w * shape[-1], (w + 1) * shape[-1]),)] for w in range(LANES)]

        def lane_sem(name):
            return [sem(f"{name}{w}") for w in range(LANES)]

        wtok = sb("wtok", [P, KC, D])
        wtok_mean = sb("wtok_mean", [P, D])
        wtok_c = sb("wtok_c", [P, KC, D])
        gain_768th = sb("gain_768th", [P, KC])
        wqc = sb("wqc", [P, PAIRS, WIDE])
        wqt = sb("wqt", [P, PAIRS, WIDE])
        wkt = sb("wkt", [P, PAIRS, ROW])
        wqk = sb("wqk", [WIDE, PAIRS, P])
        wv = sb("wv", [WIDE, 2, DC])
        rk = sb("rk", [DC, 2, PATCH])
        post = sb("post", [DC, 2, REL])
        rel = sb("rel", [P, PAIRS, REL])
        wrel = sb("wrel", [WIDE, 2, PAIRS * REL])
        wo = sb("wo", [DC, 2, D])
        wqkv = sb("wqkv", [DC, 2, 3 * D])
        wproj = [sb("wproj_large", [DC, 2, D]), sb("wproj_small", [DC, 2, D])]
        w1 = sb("w1", [DC, 2, HID])
        w2 = sb("w2", [P, HC, D])
        w2_kept = [sb(f"w2_kept{v}", [P, HC, KEEP[v]]) for v in range(3)]
        row = sb("row", [P, len(ROW_NAMES), D])
        tok_bias = sb("tok_bias", [P, D])
        bproj_small = sb("bproj_small", [P, D])
        b2_small = sb("b2_small", [P, D])
        col6 = sb("col6", [P, len(COL6_NAMES), 6])
        col2 = sb("col2", [DC, len(COL2_NAMES), 2])
        gum = sb("gum", [P, 3])
        gum_sum = sb("gum_sum", [P, 3])
        ident = sb("ident", [P, P + 2])
        norm_eps = sb("norm_eps", [P, 2])
        minus_half = sb("minus_half", [P, 2])
        zero = sb("zero", [P, 1])
        table_out = sb("table_out", [P, 1])

        def c2(name):
            return col2[:, COL2_NAMES.index(name), :]

        def vec(name):
            return row[:, ROW_NAMES.index(name), :]

        def c6(name):
            return col6[:, COL6_NAMES.index(name), :]

        xt = lane_sb("xt", [P, PATCH])
        xT_first = lane_sb("xT_first", [P, KC, P])
        xT = lane_sb("xT", [P, KC, P])
        emb_mm = lane_sb("emb_mm", [P, D])
        emb = lane_sb("emb", [P, D])
        h = lane_sb("h", [P, D])
        qn = lane_sb("qn", [P, 4, ROW])
        qn_bo = lane_sb("qn_bo", [P, D])
        h_beta = lane_sb("h_beta", [P, D])
        qnT_all, qnT = shared_sb("qnT", [WIDE, 2, P])
        qw_all, qw = shared_sb("qw", [P, PAIRS, P])
        v1 = lane_sb("v1", [P, 2, PAIRS, 2 * DV1])
        raw = lane_sb("raw", [P, RAW])
        posS = lane_sb("posS", [P, RAW])
        sc = lane_sb("sc", [P, HEADS * TOK])
        top = lane_sb("top", [P, HEADS])
        inv = lane_sb("inv", [P, HEADS])
        prob = lane_sb("prob", [P, PAIRS, 2, ROW])
        probT = lane_sb("probT", [P, PAIRS, P])
        av = lane_sb("av", [P, D])
        avT = lane_sb("avT", [DC, 2, P])
        y = lane_sb("y", [P, D])
        yc = lane_sb("yc", [P, D])
        h1 = lane_sb("h1", [P, D])
        f = lane_sb("f", [P, D])
        f_b = lane_sb("f_b", [P, D])
        nr = lane_sb("nr", [P, D])
        nT = lane_sb("nT", [DC, 2, P])
        q2 = lane_sb("q2", [DC, 2, P])
        k2 = lane_sb("k2", [DC, 2, 2, 2, TOK])
        v2 = lane_sb("v2", [P, 2, PAIRS, 2 * DV1])
        f2 = lane_sb("f2", [P, D])
        nr2 = lane_sb("nr2", [P, D])
        n2T_all, n2T = shared_sb("n2T", [DC, 2, P])
        hid_all, hid = shared_sb("hid", [P, 3 * GROUPS, CHUNK, P])
        rest = lane_sb("rest", [P, D])
        h1_b = lane_sb("h1_b", [P, D])
        res = lane_sb("res", [P, D])
        stats = lane_sb("stats", [P, 2, 6])
        mv = lane_sb("mv", [P, FRONT_LN + BACK_LN, 2])
        var_eps = lane_sb("var_eps", [P, FRONT_LN + BACK_LN, 2])
        rstd = lane_sb("rstd", [P, FRONT_LN + BACK_LN, 2])
        scratch = [nc.dram_tensor(f"raw_scores{w}", [P, RAW], F32).ap() for w in range(LANES)]

        ps = [ctx.enter_context(nc.psum_tensor(f"ps{w}", [P, 4, 512], F32)) for w in range(LANES)]

        tok_loaded = sem("tok_loaded")
        early_loaded = sem("early_loaded")
        keys_loaded = sem("keys_loaded")
        rel_loaded = sem("rel_loaded")
        ffn_loaded = sem("ffn_loaded")
        xt_zeroed = sem("xt_zeroed")
        posS_zeroed = sem("posS_zeroed")
        zeroed_v = sem("zeroed_v")
        zeroed_p = sem("zeroed_p")
        zeroed_a = sem("zeroed_a")
        setup_mm = sem("setup_mm")
        bias_read = sem("bias_read")
        rel_mm = sem("rel_mm")
        rel_ready = sem("rel_ready")
        setup_v = sem("setup_v")
        setup_p = sem("setup_p")
        dve_chain = sem("dve_chain")
        pool_chain = sem("pool_chain")
        x_loaded = lane_sem("x_loaded")
        first_loaded = lane_sem("first_loaded")
        xT_loaded = lane_sem("xT_loaded")
        tok_mm = lane_sem("tok_mm")
        emb_ready = lane_sem("emb_ready")
        h_ready = lane_sem("h_ready")
        qn_ready = lane_sem("qn_ready")
        qnT_mm = lane_sem("qnT_mm")
        qnT_ready = lane_sem("qnT_ready")
        q_mm = sem("q_mm")
        qw_ready = sem("qw_ready")
        pos_mm = lane_sem("pos_mm")
        raw_ready = lane_sem("raw_ready")
        raw_stored = lane_sem("raw_stored")
        pos_loaded = lane_sem("pos_loaded")
        score_mm = [lane_sem("score_mm_a"), lane_sem("score_mm_b")]
        sc_ready = [lane_sem("sc_ready_a"), lane_sem("sc_ready_b")]
        prob_ready = [lane_sem("prob_ready_a"), lane_sem("prob_ready_b")]
        v_mm = [lane_sem("v_mm_a"), lane_sem("v_mm_b")]
        v_ready = [lane_sem("v_ready_a"), lane_sem("v_ready_b")]
        pT_mm = [lane_sem("pT_mm_a"), lane_sem("pT_mm_b")]
        pT_ready_act = [lane_sem("pT_act_a"), lane_sem("pT_act_b")]
        pT_ready_dve = [lane_sem("pT_dve_a"), lane_sem("pT_dve_b")]
        pv_mm = [lane_sem("pv_mm_a"), lane_sem("pv_mm_b")]
        av_ready = [lane_sem("av_ready_a"), lane_sem("av_ready_b")]
        avT_mm = [lane_sem("avT_mm_a"), lane_sem("avT_mm_b")]
        avT_ready = [lane_sem("avT_ready_a"), lane_sem("avT_ready_b")]
        o_mm = [lane_sem("o_mm_a"), lane_sem("o_mm_b")]
        front_var = lane_sem("front_var")
        front_rstd = lane_sem("front_rstd")
        back_var = lane_sem("back_var")
        back_rstd = lane_sem("back_rstd")
        qn_bo_ready = lane_sem("qn_bo_ready")
        h_beta_ready = lane_sem("h_beta_ready")
        h1_ready = lane_sem("h1_ready")
        f_ready = lane_sem("f_ready")
        f_b_ready = lane_sem("f_b_ready")
        nr_ready = lane_sem("nr_ready")
        nT_mm = lane_sem("nT_mm")
        nT_ready = lane_sem("nT_ready")
        q2_mm = lane_sem("q2_mm")
        q2_ready = lane_sem("q2_ready")
        k2_mm = lane_sem("k2_mm")
        k2_ready = lane_sem("k2_ready")
        f2_ready = lane_sem("f2_ready")
        nr2_ready = lane_sem("nr2_ready")
        n2T_mm = lane_sem("n2T_mm")
        n2T_ready = lane_sem("n2T_ready")
        n2T_ready_dve = lane_sem("n2T_ready_dve")
        fc1_mm = sem("fc1_mm")
        gelu_ready = sem("gelu_ready")
        fc2_mm = lane_sem("fc2_mm")
        rest_ready = lane_sem("rest_ready")
        res_ready = lane_sem("res_ready")
        res_free = lane_sem("res_free")

        BOTH = LANES * 2 * TOK
        Q_BANKS = (1, 2, 0)
        MLP_BANKS = ((0, 1), (0, 2), (1, 1))
        FRONT = 3
        TOK_LOADED = 16 * 2
        WARM_PLACES = ("first_probs0", "first_probs1",
                       "first_projection",
                       "second_probs0", "second_probs1",
                       "second_projection",
                       "norm_turned",
                       "content_scores",
                       "values")
        WARM = ((0, 0, 1, 8, 0, 6, 2, 2, 6), (4, 4, 4, 6, 0, 8, 3, 4, 2), (4, 6, 10, 6, 2, 8, 3, 4, 2))
        EARLY = 16 * 3
        KEYS_LOADED = 16 * 2
        REL_LOADED = 16 * 5
        FFN_LOADED = 16 * 5
        ZEROED_V = 2

        def chunks(small):
            return [(v, c) for v in ((2, 1, 0) if small else (0,)) for c in range(0, HC, CHUNK)]

        def chunk_count(n, j, small):
            large = len(chunks(False))
            if not small:
                return n * large + (j + 1)
            per = len(chunks(True))
            return n * per + (LARGE_STEPS * (large - per) + j + 1)

        def blocks(ap):
            return ap.rearrange("p (x t) -> p x t", t=ROW)[:, :, 0:TOK]

        def queries(i):
            return (blocks(qw_all[:, 2 * i:2 * i + 2, :].rearrange("p m t -> p (m t)")),
                    ps[0][:, Q_BANKS[i], 0:2 * BOTH].rearrange("p (x t) -> p x t", t=TOK))

        def turned(ap):
            return ap.rearrange("p (c t) -> p c t", t=P)[:, :, 0:ROWS]

        block = ctx.enter_context(nc.Block())

        @block.sync
        def _(sp):
            def load_x(m, w):
                for b in range(2):
                    sp.dma_start(xt[w][b * ROW:b * ROW + TOK, :], x[m, w, b]).then_inc(x_loaded[w], 16)

            def shift(m):
                for w in lanes:
                    sp.wait_ge(raw_ready[w], 4 * m + 4)
                    sp.dma_start(scratch[w][0:ROW + TOK, :], raw[w][0:ROW + TOK, :]).then_inc(raw_stored[w], 16)
                for w in lanes:
                    sp.wait_ge(raw_stored[w], 16 * m + 16)
                    for b in range(2):
                        skewed = bass.AP(scratch[w].tensor, b * ROW * RAW + TOK - 1, [[RAW - 1, TOK], [1, SHIFTED]])
                        sp.dma_start(posS[w][b * ROW:b * ROW + TOK, 0:SHIFTED], skewed).then_inc(pos_loaded[w], 16)

            def refill(m):
                for w in lanes:
                    sp.wait_ge(tok_mm[w], m)
                    sp.dma_start(xT[w][:], x_t[m, w]).then_inc(xT_loaded[w], 16)
                for w in lanes:
                    sp.wait_ge(front_var[w], FRONT_LN * (m - 1) + 1)
                    load_x(m, w)

            def store(n, w):
                sp.wait_ge(res_ready[w], n + 2)
                for b in range(2):
                    sp.dma_start(out[n, w, b], res[w][b * ROW:b * ROW + TOK, :]).then_inc(res_free[w], 16)

            lanes = range(LANES)
            sp.dma_start(wtok[:], w_tok).then_inc(tok_loaded, 16)
            for w in lanes:
                sp.dma_start(xT_first[w][:], x_t[0, w]).then_inc(first_loaded[w], 16)
            for w in lanes:
                sp.wait_ge(xt_zeroed, w + 1)
                load_x(0, w)
            for dst, src in ((wqt, w_qt), (wqc, w_qc), (wkt, w_kt), (wv, w_v), (wo, w_o)):
                sp.dma_start(dst[:], src).then_inc(rel_loaded, 16)
            for w in lanes:
                sp.dma_start(xT[w][:], x_t[1, w]).then_inc(xT_loaded[w], 16)
            for dst, src in ((col2, cols2), (wqkv, w_qkv), (wproj[0], w_proj), (w1, w_fc1), (w2, w_fc2)):
                sp.dma_start(dst[:], src).then_inc(ffn_loaded, 16)
            sp.wait_ge(posS_zeroed, LANES)
            for w in lanes:
                sp.wait_ge(front_var[w], 1)
                load_x(1, w)
            refill(2)
            shift(0)
            for n in range(STEPS):
                if n + 1 < STEPS:
                    shift(n + 1)
                if n + 3 < STEPS:
                    refill(n + 3)
                for w in lanes:
                    store(n, w)
            for w in lanes:
                sp.wait_ge(res_free[w], 32 * STEPS + 32)

        @block.gpsimd
        def _(pool):
            chain = [0]

            def link(ins):
                chain[0] += 1
                ins.then_inc(pool_chain, 1)
                pool.wait_ge(pool_chain, chain[0])

            def restart():
                pool.sem_clear(pool_chain)
                chain[0] = 0

            for w in range(LANES):
                for values in (v1[w], v2[w]):
                    link(pool.memset(values[:], 0.0))
                    for r in range(2):
                        link(pool.memset(values[r * ROW:(r + 1) * ROW, :, :, r * DV1 + DV], 1.0))
                pool.memset(prob[w][:, :, :, TOK:ROW], 0.0)
            pool.memset(hid_all[:].rearrange("p j c (x t) -> p (j c x) t", t=ROW)[:, :, TOK:ROW],
                        0.0).then_inc(zeroed_p, 1)

            def moment(m, w, i):
                front = i < FRONT_LN
                var, done = (front_var, front_rstd) if front else (back_var, back_rstd)
                k = i if front else i - FRONT_LN
                pool.wait_ge(var[w], (FRONT_LN if front else BACK_LN) * m + (k + 1))
                return mv[w][:, i, 1:2], done[w]

            def rsqrt(m, w, i):
                var, done = moment(m, w, i)
                eps = norm_eps[:, 1:2] if i == ATTN_LN else norm_eps[:, 0:1]
                link(pool.tensor_tensor(var_eps[w][:, i, 0:1], var, eps, ALU.add))
                pool.tensor_tensor(rstd[w][:, i, 0:1], var_eps[w][:, i, 0:1], minus_half[:, 0:1],
                                   ALU.pow).then_inc(done, 1)

            def rsqrt_twice(m, w, i):
                var, done = moment(m, w, i)
                pool.tensor_tensor(var_eps[w][:, i, 0:1], var, norm_eps[:, 0:1], ALU.add)
                link(pool.tensor_scalar(var_eps[w][:, i, 1:2], var, 1.0 + EPS, EPS * EPS, ALU.mult, ALU.add))
                pool.tensor_tensor(rstd[w][:, i, :], var_eps[w][:, i, :], minus_half[:], ALU.pow).then_inc(done, 1)

            def front_a(m):
                for i in (1, 2):
                    for w in lanes:
                        rsqrt(m, w, i)

            def front_b(m):
                for w in lanes:
                    pool.wait_ge(h_ready[w], m + 1)
                    pool.tensor_tensor(h_beta[w][:], h[w][:], vec("beta"), ALU.add).then_inc(h_beta_ready[w], 1)
                    pool.wait_ge(qn_ready[w], m + 1)
                    pool.tensor_tensor(qn_bo[w][:].rearrange("p (g d) -> p g d", g=4), qn[w][:, :, 0:FEAT],
                                       vec("bo").rearrange("p (g d) -> p g d", g=4), ALU.add).then_inc(qn_bo_ready[w], 1)

            def step(n, small, ahead):
                restart()
                for w in lanes:
                    rsqrt(n, w, 3)
                    rsqrt_twice(n, w, 4)
                for w in lanes:
                    pool.wait_ge(h1_ready[w], n + 1)
                    link(pool.tensor_tensor(h1_b[w][:], h1[w][:], b2_small[:] if small else vec("b_fc2"), ALU.add))
                    pool.wait_ge(f_ready[w], n + 1)
                    pool.tensor_tensor(f_b[w][:], f[w][:], bproj_small[:] if small else vec("b_proj"),
                                       ALU.add).then_inc(f_b_ready[w], 1)
                if ahead:
                    front_b(n + 1)
                for w in lanes:
                    rsqrt(n, w, 5)
                for w in lanes:
                    pool.wait_ge(f2_ready[w], n + 1)
                    pool.tensor_tensor(rest[w][:], h1_b[w][:], f2[w][:], ALU.add).then_inc(rest_ready[w], 1)
                if not small:
                    for w in lanes:
                        rsqrt(n + 2, w, 0)
                    front_a(n + 2)

            def small_setup():
                restart()

                def times(dst, src, g):
                    link(pool.tensor_scalar(dst, src, g, 1.0, ALU.mult, ALU.mult))

                link(pool.tensor_tensor(gum_sum[:, 0:1], gum[:, 0:1], zero[:], ALU.add))
                link(pool.tensor_tensor(gum_sum[:, 1:2], gum_sum[:, 0:1], gum[:, 1:2], ALU.add))
                link(pool.tensor_tensor(gum_sum[:, 2:3], gum_sum[:, 1:2], gum[:, 2:3], ALU.add))
                pool.wait_ge(ffn_loaded, FFN_LOADED)
                cuts = ((0, KEEP[2], 2), (KEEP[2], KEEP[1], 1), (KEEP[1], D, 0))
                for a, b, g in cuts:
                    times(bproj_small[:, a:b], vec("b_proj")[:, a:b], gum_sum[:, g:g + 1])
                    times(b2_small[:, a:b], vec("b_fc2")[:, a:b], gum_sum[:, g:g + 1])
                for a, b, g in cuts:
                    times(wproj[1][0:KEEP[2], 0, a:b], wproj[0][0:KEEP[2], 0, a:b], gum_sum[0:KEEP[2], g:g + 1])
                for a, b, g in ((0, KEEP[1], 1), (KEEP[1], D, 0)):
                    times(wproj[1][KEEP[2]:DC, 0, a:b], wproj[0][KEEP[2]:DC, 0, a:b], gum_sum[KEEP[2]:DC, g:g + 1])
                times(wproj[1][:, 1, :], wproj[0][:, 1, :], gum_sum[0:DC, 0:1])
                for v in range(2):
                    times(w2_kept[v][:], w2[:, :, 0:KEEP[v]], gum[:, v:v + 1])
                pool.tensor_scalar(w2_kept[2][:], w2[:, :, 0:KEEP[2]], gum[:, 2:3], 1.0, ALU.mult,
                                   ALU.mult).then_inc(setup_p, 1)

            lanes = range(LANES)
            pool.wait_ge(early_loaded, EARLY)
            pool.wait_ge(zeroed_v, ZEROED_V)
            restart()
            for w in lanes:
                rsqrt(0, w, 0)
            front_a(0)
            front_b(0)
            for w in lanes:
                rsqrt(1, w, 0)
            front_a(1)
            small_setup()
            with pool.Fori(0, LARGE_STEPS) as n:
                step(n, False, True)
            step(LARGE_STEPS, True, True)
            step(LARGE_STEPS + 1, True, False)

        @block.scalar
        def _(act):
            lanes = range(LANES)

            def zero_psum(w):
                act.activation(ps[w][:].rearrange("p b c -> p (b c)"), zero[:].to_broadcast([P, 4 * 512]),
                               ACT.Copy).then_inc(zeroed_a, 1)

            act.dma_start(col6[:], cols6).then_inc(tok_loaded, 16)
            act.wait_ge(zeroed_v, 1)
            zero_psum(0)
            for dst, src in ((rk, r_kernel), (post, pos_t)):
                act.dma_start(dst[:], src).then_inc(keys_loaded, 16)
            for dst, src in ((row, bass.AP(rows.tensor, 0, [[0, P], [D, len(ROW_NAMES)], [1, D]])),
                             (ident, ident_in), (gum, bass.AP(gumbel.tensor, 0, [[0, P], [1, 3]]))):
                act.dma_start(dst[:], src).then_inc(early_loaded, 16)
            zero_psum(1)

            def transposed_probs(n, w, a):
                act.wait_ge(pT_mm[a][w], n + 1)
                act.activation(probT[w][:, 0:3, 0:ROWS], turned(ps[w][:, 0, 0:384]), ACT.Copy).then_inc(pT_ready_act[a][w], 1)

            def exp_scores(n, w, a):
                act.wait_ge(sc_ready[a][w], n + 1)
                if a == 0:
                    dst = prob[w][:, :, :, 0:TOK].rearrange("p m r t -> p r m t")
                    src = sc[w][:].rearrange("p (r m t) -> p r m t", r=2, t=TOK)
                else:
                    dst = prob[w][:, :, :, 0:TOK].rearrange("p m r t -> p (m r) t")
                    src = sc[w][:].rearrange("p (n t) -> p n t", t=TOK)
                act.activation(dst, src, ACT.Exp).then_inc(prob_ready[a][w], 1)

            def transposed_av(n, w, a):
                act.wait_ge(avT_mm[a][w], n + 1)
                act.activation(avT[w][:, :, 0:ROWS], turned(ps[w][0:DC, 1, 0:2 * P]), ACT.Copy).then_inc(avT_ready[a][w], 1)

            def affine_columns(n, w, done, dst, gain, shift, ready, of):
                act.wait_ge(done[w], n + 1)
                for c in of:
                    last = act.activation(dst[w][:, c, 0:ROWS], ps[w][0:DC, 1, c * P:c * P + ROWS], ACT.Identity,
                                          scale=gain[:, c:c + 1], bias=shift[:, c:c + 1])
                last.then_inc(ready[w], 1)

            def front_embed(m, of=range(LANES), bank=FRONT):
                for w in of:
                    act.wait_ge(tok_mm[w], m + 1)
                    act.activation(emb_mm[w][:], ps[w][:, bank, 0:D], ACT.Copy).then_inc(emb_ready[w], 1)

            def front_queries(m):
                for w in lanes:
                    act.wait_ge(qnT_mm[w], m + 1)
                    act.activation(qnT[w][:, :, 0:ROWS], turned(ps[w][0:WIDE, FRONT, 0:2 * P]), ACT.Copy).then_inc(qnT_ready[w], 1)

            def raw_scores(m, g):
                for w in lanes:
                    act.wait_ge(pos_mm[w], 4 * m + (g + 1))
                    act.activation(raw[w][:, g * 3 * REL:(g + 1) * 3 * REL], ps[w][:, FRONT, 0:3 * REL],
                                   ACT.Copy).then_inc(raw_ready[w], 1)

            def step(n, small, ahead):
                size = "s" if small else "l"
                act.wait_ge(q_mm, 3 * n + 2)
                act.activation(*queries(1), ACT.Copy).then_inc(qw_ready, 1)
                for w in lanes:
                    exp_scores(n, w, 0)
                    if w == 0 and not small:
                        front_embed(n + 2, (0,))
                    transposed_probs(n, w, 0)
                if not small:
                    front_embed(n + 2, (1,))
                for w in lanes:
                    transposed_av(n, w, 0)
                if ahead:
                    front_queries(n + 1)
                    raw_scores(n + 1, 0)
                    raw_scores(n + 1, 1)
                for w in lanes:
                    affine_columns(n, w, nT_mm, nT, c2(f"n1{size}_g"), c2(f"n1{size}_b"), nT_ready, (0, 1))
                for w in lanes:
                    exp_scores(n, w, 1)
                    if ahead and w == 1:
                        raw_scores(n + 1, 2)
                    transposed_probs(n, w, 1)
                for w in lanes:
                    transposed_av(n, w, 1)
                act.activation(table_out[:], zero[:], ACT.Gelu)
                if ahead:
                    raw_scores(n + 1, 3)
                for w in lanes:
                    affine_columns(n, w, n2T_mm, n2T, c2(f"n2{size}_g"), c2(f"n2{size}_b"), n2T_ready, (0,))
                for j, (v, c) in enumerate(chunks(small)):
                    act.wait_ge(fc1_mm, chunk_count(n, j, small))
                    w, bank = MLP_BANKS[j % GROUPS]
                    for i in range(CHUNK):
                        last = act.activation(
                            blocks(hid_all[:, j, i, :]),
                            ps[w][:, bank, i * BOTH:(i + 1) * BOTH].rearrange("p (x t) -> p x t", t=TOK),
                            ACT.Gelu, bias=c6("b_fc1")[:, c + i:c + i + 1])
                    last.then_inc(gelu_ready, 1)

            act.wait_ge(rel_mm, 1)
            for r in range(2):
                last = act.activation(rel[:, 3 * r:3 * r + 3, :], ps[1][:, r, 0:3 * REL], ACT.Copy)
            last.then_inc(rel_ready, 1)
            front_embed(0)
            act.wait_ge(rel_mm, 2)
            for r in range(2):
                for c in range(2):
                    last = act.activation(wrel[:, c, :].rearrange("p (m r t) -> p m r t", r=2, t=REL)[:, :, r, :],
                                          ps[r][0:WIDE, c, 0:3 * REL].rearrange("p (m t) -> p m t", t=REL),
                                          ACT.Copy, scale=SCALE)
            last.then_inc(rel_ready, 1)
            act.wait_ge(rel_mm, 3)
            for r in range(2):
                last = act.activation(wqk[:, :, r * ROW:(r + 1) * ROW],
                                      ps[r][0:WIDE, 2, 0:PAIRS * ROW].rearrange("p (m t) -> p m t", t=ROW),
                                      ACT.Copy, scale=SCALE)
            last.then_inc(rel_ready, 1)

            def first_ahead(w):
                act.wait_ge(front_var[w], 2)
                front_embed(1, (w,), 1)

            first_ahead(0)
            front_queries(0)
            raw_scores(0, 0)
            first_ahead(1)
            for g in range(1, 4):
                raw_scores(0, g)
            act.wait_ge(ffn_loaded, FFN_LOADED)
            act.wait_ge(zeroed_p, 1)
            with act.Fori(0, LARGE_STEPS) as n:
                step(n, False, True)
            step(LARGE_STEPS, True, True)
            step(LARGE_STEPS + 1, True, False)

        @block.vector
        def _(dve):
            lanes = range(LANES)
            chain = [0]

            def link(ins):
                chain[0] += 1
                ins.then_inc(dve_chain, 1)
                dve.wait_ge(dve_chain, chain[0])

            def restart():
                dve.sem_clear(dve_chain)
                chain[0] = 0

            dve.memset(zero[:], 0.0).then_inc(zeroed_v, 1)
            for w in lanes:
                dve.memset(xt[w][:], 0.0).then_inc(xt_zeroed, 1)
            dve.memset(norm_eps[:, 0:1], EPS)
            dve.memset(norm_eps[:, 1:2], EPS_ATTN)
            dve.memset(minus_half[:], -0.5).then_inc(zeroed_v, 1)
            dve.wait_ge(tok_loaded, TOK_LOADED)
            dve.tensor_scalar(gain_768th[:], c6("ln1_g"), 1.0 / PATCH, None, ALU.mult).then_inc(setup_v, 1)
            for w in lanes:
                dve.memset(res[w][:, 0:DC], 0.0).then_inc(res_free[w], 32)
                dve.memset(res[w][:, DC:D], 0.0).then_inc(res_ready[w], 1)
                dve.memset(posS[w][:], 0.0).then_inc(posS_zeroed, 1)
                dve.memset(qn[w][:, :, FEAT:FEAT + 1], 1.0)
                dve.memset(qn[w][:, :, FEAT + 1:ROW], 0.0)
                dve.memset(inv[w][:], 1.0)

            def fold():
                dve.wait_ge(setup_mm, 1)
                link(dve.tensor_copy(wtok_mean[:], ps[0][:, 0, 0:D]))
                for c in range(KC):
                    last = dve.scalar_tensor_tensor(out=wtok_c[:, c, :], in0=wtok[:, c, :], scalar=c6("ln1_g")[:, c:c + 1],
                                                    in1=wtok_mean[:], op0=ALU.mult, op1=ALU.subtract)
                last.then_inc(setup_v, 1)
                dve.wait_ge(setup_mm, 2)
                dve.wait_ge(early_loaded, EARLY)
                dve.tensor_tensor(tok_bias[:], ps[0][:, 1, 0:D], vec("tok_b"), ALU.add).then_inc(bias_read, 1)
                dve.wait_ge(bias_read, 1)

            def moments(w, i, src):
                k = src.shape[1] // 384 or 1
                size = src.shape[1] // k
                for j in range(k):
                    last = dve.bn_stats(stats[w][:, j, :], src[:, j * size:(j + 1) * size])
                link(last)
                var = (front_var if i < FRONT_LN else back_var)[w]
                dve.bn_aggr(mv[w][:, i, :], stats[w][:, 0:k, :]).then_inc(var, 1)

            def mean(w, i):
                return mv[w][:, i, 0:1]

            def inv_dev(w, i, twice=0):
                return rstd[w][:, i, twice:twice + 1]

            def rstd_done(m, w, i):
                if i < FRONT_LN:
                    dve.wait_ge(front_rstd[w], m * FRONT_LN + (i + 1))
                else:
                    dve.wait_ge(back_rstd[w], m * BACK_LN + (i - FRONT_LN + 1))

            def normalise(m, w, i, src, dst, twice=0):
                rstd_done(m, w, i)
                return dve.tensor_scalar(dst, src, mean(w, i), inv_dev(w, i, twice), ALU.subtract, ALU.mult)

            def normalise_affine(m, w, i, src, gain, shift, dst):
                centre(m, w, i, src, gain)
                return scale_shift(m, w, i, shift, dst)

            def centre(m, w, i, src, gain):
                if i < FRONT_LN:
                    dve.wait_ge(front_var[w], m * FRONT_LN + (i + 1))
                else:
                    dve.wait_ge(back_var[w], m * BACK_LN + (i - FRONT_LN + 1))
                link(dve.scalar_tensor_tensor(out=yc[w][:], in0=src, scalar=mean(w, i), in1=gain,
                                              op0=ALU.subtract, op1=ALU.mult))

            def scale_shift(m, w, i, shift, dst):
                rstd_done(m, w, i)
                return dve.scalar_tensor_tensor(out=dst, in0=yc[w][:], scalar=inv_dev(w, i), in1=shift,
                                                op0=ALU.mult, op1=ALU.add)

            def per_head(ap):
                return ap.unsqueeze(2).to_broadcast([P, HEADS, TOK])

            def softmax_front(n, w, a):
                softmax_top(n, w, a)
                softmax_less(w, a)

            def softmax_top(n, w, a):
                flat = sc[w][:].rearrange("p (n t) -> p n t", t=TOK)
                if a == 0:
                    dve.wait_ge(pos_loaded[w], 32 * n + 32)
                    dve.wait_ge(score_mm[0][w], n + 1)
                    link(dve.tensor_tensor(
                        sc[w][:].rearrange("p (r m t) -> p r m t", r=2, t=TOK),
                        ps[w][:, 1:3, 0:PAIRS * TOK].rearrange("p r (m t) -> p r m t", t=TOK),
                        posS[w][:].rearrange("p (m r t) -> p r m t", r=2, t=REL)[:, :, :, 0:TOK], ALU.add))
                    src, top_src = flat, flat
                    top_dst = top[w][:]
                else:
                    dve.wait_ge(score_mm[1][w], n + 1)
                    src = ps[w][:, 0:3, 0:4 * TOK].rearrange("p g (q t) -> p g q t", t=TOK)
                    top_src, top_dst = src, top[w][:].rearrange("p (g q) -> p g q", g=3)
                link(dve.tensor_reduce(top_dst, top_src, AX_X, ALU.max))

            def softmax_less(w, a):
                if a == 0:
                    flat = sc[w][:].rearrange("p (n t) -> p n t", t=TOK)
                    last = dve.tensor_tensor(flat, flat, per_head(top[w][:]), ALU.subtract)
                else:
                    last = dve.tensor_tensor(
                        sc[w][:].rearrange("p (g q t) -> p g q t", g=3, t=TOK),
                        ps[w][:, 0:3, 0:4 * TOK].rearrange("p g (q t) -> p g q t", t=TOK),
                        top[w][:].rearrange("p (g q) -> p g q", g=3).unsqueeze(3).to_broadcast([P, 3, 4, TOK]),
                        ALU.subtract)
                last.then_inc(sc_ready[a][w], 1)

            def values(n, w, a):
                dst = (v1, v2)[a][w]
                dve.wait_ge(v_mm[a][w], n + 1)
                for r in range(2):
                    rows_ = slice(r * ROW, (r + 1) * ROW)
                    o = dst[rows_, :, :, r * DV1:r * DV1 + DV]
                    i = ps[w][rows_, 0, 0:D].rearrange("p (b m d) -> p b m d", b=2, d=DV)
                    last = dve.tensor_copy(o, i)
                last.then_inc(v_ready[a][w], 1)

            def transposed_probs(n, w, a):
                dve.wait_ge(pT_mm[a][w], n + 1)
                dve.tensor_copy(probT[w][:, 3:6, 0:ROWS], turned(ps[w][:, 1, 0:384])).then_inc(
                    pT_ready_dve[a][w], 1)

            def attended(n, w, a):
                dve.wait_ge(pv_mm[a][w], n + 1)
                sums = ps[w][:, 2, 0:HEADS * DV1].rearrange("p (n d) -> p n d", d=DV1)
                for b in range(2):
                    toks = slice(b * ROW, b * ROW + TOK)
                    last = dve.reciprocal(inv[w][toks, :], sums[toks, :, DV])
                link(last)
                dve.tensor_tensor(av[w][:].rearrange("p (n d) -> p n d", d=DV), sums[:, :, 0:DV],
                                  inv[w][:].unsqueeze(2).to_broadcast([P, HEADS, DV]),
                                  ALU.mult).then_inc(av_ready[a][w], 1)

            def attention_sum(n, w):
                dve.wait_ge(qn_bo_ready[w], n + 1)
                dve.wait_ge(o_mm[0][w], n + 1)
                link(dve.tensor_tensor(y[w][:], ps[w][:, 0, 0:D], qn_bo[w][:], ALU.add))
                moments(w, 3, y[w][:])
                centre(n, w, 3, y[w][:], vec("gamma"))

            def hidden(n, w):
                dve.wait_ge(h_beta_ready[w], n + 1)
                scale_shift(n, w, 3, h_beta[w][:], h1[w][:]).then_inc(h1_ready[w], 1)
                dve.wait_ge(h1_ready[w], n + 1)
                moments(w, 4, h1[w][:])

            def twice_normalised(n, w):
                normalise(n, w, 4, h1[w][:], nr[w][:], twice=1).then_inc(nr_ready[w], 1)

            def once_normalised(n, w):
                normalise(n, w, 4, h1[w][:], f[w][:]).then_inc(f_ready[w], 1)

            def second_chunk(n, w, size):
                dve.wait_ge(n2T_mm[w], n + 1)
                dve.tensor_scalar(n2T[w][:, 1, 0:ROWS], ps[w][0:DC, 0, 0:ROWS], c2(f"n2{size}_g")[:, 1:2],
                                  c2(f"n2{size}_b")[:, 1:2], ALU.mult, ALU.add).then_inc(n2T_ready_dve[w], 1)

            def front_patch(m, w):
                dve.wait_ge(x_loaded[w], 32 * m + 32)
                moments(w, 0, xt[w][:])

            def front_embed(m):
                for w in lanes:
                    dve.wait_ge(emb_ready[w], m + 1)
                    rstd_done(m, w, 0)
                    link(dve.scalar_tensor_tensor(out=emb[w][:], in0=emb_mm[w][:], scalar=inv_dev(w, 0),
                                                  in1=tok_bias[:], op0=ALU.mult, op1=ALU.add))
                    moments(w, 1, emb[w][:])

            def front_h(m, first=False):
                for w in lanes:
                    if not first:
                        dve.wait_ge(h_beta_ready[w], m)
                    normalise_affine(m, w, 1, emb[w][:], vec("ln2_g"), vec("ln2_b"), h[w][:]).then_inc(h_ready[w], 1)
                    dve.wait_ge(h_ready[w], m + 1)
                    moments(w, 2, h[w][:])

            def front_query(m, first=False):
                for w in lanes:
                    if not first:
                        dve.wait_ge(qn_bo_ready[w], m)
                        dve.wait_ge(qnT_mm[w], m)
                    normalise(m, w, 2, h[w][:].rearrange("p (g d) -> p g d", g=4),
                              qn[w][:, :, 0:FEAT]).then_inc(qn_ready[w], 1)

            def step(n, small, ahead):
                size = "s" if small else "l"
                restart()
                for i in (0, 2):
                    dve.wait_ge(q_mm, 3 * n + (i + 1))
                    dve.tensor_copy(*queries(i)).then_inc(qw_ready, 1)
                for w in lanes:
                    values(n, w, 0)
                softmax_front(n, 0, 0)
                softmax_top(n, 1, 0)
                transposed_probs(n, 0, 0)
                softmax_less(1, 0)
                attended(n, 0, 0)
                transposed_probs(n, 1, 0)
                attended(n, 1, 0)
                attention_sum(n, 0)
                hidden(n, 0)
                attention_sum(n, 1)
                twice_normalised(n, 0)
                hidden(n, 1)
                once_normalised(n, 0)
                twice_normalised(n, 1)
                once_normalised(n, 1)
                for w in lanes:
                    dve.wait_ge(q2_mm[w], n + 1)
                    dve.tensor_scalar(q2[w][:].rearrange("p c (b t) -> p c b t", b=2)[:, :, :, 0:TOK],
                                      ps[w][0:DC, 2, 0:4 * TOK].rearrange("p (c b t) -> p c b t", c=2, b=2),
                                      SCALE_FFN, None, ALU.mult).then_inc(q2_ready[w], 1)
                    dve.wait_ge(k2_mm[w], n + 1)
                    for r in range(2):
                        last = dve.tensor_scalar(k2[w][:, :, :, r, :],
                                                 ps[w][0:DC, 1, 0:4 * TOK].rearrange("p (c b t) -> p c b t", c=2, b=2),
                                                 ident[0:DC, P + r:P + r + 1], None, ALU.mult)
                    last.then_inc(k2_ready[w], 1)
                    values(n, w, 1)
                for w in lanes:
                    softmax_front(n, w, 1)
                for w in lanes:
                    transposed_probs(n, w, 1)
                for w in lanes:
                    attended(n, w, 1)
                for w in lanes:
                    dve.wait_ge(f_b_ready[w], n + 1)
                    dve.wait_ge(o_mm[1][w], n + 1)
                    dve.tensor_tensor(f2[w][:], ps[w][:, 0, 0:D], f_b[w][:], ALU.add).then_inc(f2_ready[w], 1)
                    dve.wait_ge(f2_ready[w], n + 1)
                    moments(w, 5, f2[w][:])
                    if w > 0:
                        normalise(n, w - 1, 5, f2[w - 1][:], nr2[w - 1][:]).then_inc(nr2_ready[w - 1], 1)
                w = LANES - 1
                normalise(n, w, 5, f2[w][:], nr2[w][:]).then_inc(nr2_ready[w], 1)
                for w in lanes:
                    second_chunk(n, w, size)
                if not small:
                    for w in lanes:
                        front_patch(n + 2, w)
                    front_embed(n + 2)
                    front_h(n + 2)
                    front_query(n + 2)
                for w in lanes:
                    dve.wait_ge(rest_ready[w], n + 1)
                    dve.wait_ge(res_free[w], 32 * n + 32)
                    dve.wait_ge(fc2_mm[w], n + 1)
                    dve.tensor_tensor(res[w][:], ps[w][:, 0, 0:D], rest[w][:], ALU.add).then_inc(res_ready[w], 1)

            fold()
            restart()
            for w in lanes:
                front_patch(0, w)
            front_embed(0)
            front_h(0, first=True)
            front_query(0, first=True)
            for w in lanes:
                front_patch(1, w)
            front_embed(1)
            front_h(1)
            front_query(1)
            with dve.Fori(0, LARGE_STEPS) as n:
                step(n, False, True)
            step(LARGE_STEPS, True, True)
            step(LARGE_STEPS + 1, True, False)

        @block.tensor
        def _(pe):
            lanes = range(LANES)

            def chunk_each(src, w):
                for c in range(2):
                    last = pe.transpose(ps[w][0:DC, 1 - c, 0:ROWS], src[w][0:ROWS, c * DC:(c + 1) * DC],
                                        ident[0:ROWS, 0:ROWS])
                return last

            def features(src, w):
                def into(bank):
                    for c in range(2):
                        last = pe.transpose(ps[w][0:DC, bank, c * P:c * P + ROWS], src[w][0:ROWS, c * DC:(c + 1) * DC],
                                            ident[0:ROWS, 0:ROWS])
                    return last
                return into

            def every_other(weights, r):
                return weights.rearrange("p (m r d) -> p m r d", r=2, d=DV)[:, :, r, :]

            def tokens(srcT, w, c):
                return blocks(srcT[w][:, c, :])

            def back(n, w, a, weights):
                vals = (v1, v2)[a][w]

                def transposes():
                    pe.wait_ge(prob_ready[a][w], n + 1)
                    pe.wait_ge(v_ready[a][w], n + 1)
                    for m in range(PAIRS):
                        last = pe.transpose(ps[w][:, m // 3, (m % 3) * P:(m % 3) * P + ROWS],
                                            prob[w][0:ROWS, m, :, :].rearrange("p r t -> p (r t)"),
                                            ident[0:ROWS, 0:ROWS])
                    last.then_inc(pT_mm[a][w], 1)

                def attend():
                    pe.wait_ge(pT_ready_act[a][w], n + 1)
                    pe.wait_ge(pT_ready_dve[a][w], n + 1)
                    for b in range(2):
                        for m in range(PAIRS):
                            last = pe.matmul(ps[w][b * ROW:b * ROW + TOK, 2, m * 2 * DV1:(m + 1) * 2 * DV1],
                                             probT[w][:, m, b * ROW:b * ROW + TOK], vals[:, b, m, :],
                                             start=True, stop=True)
                    last.then_inc(pv_mm[a][w], 1)

                def turn():
                    pe.wait_ge(av_ready[a][w], n + 1)
                    features(av, w)(1).then_inc(avT_mm[a][w], 1)

                def project():
                    pe.wait_ge(avT_ready[a][w], n + 1)
                    for c in range(2):
                        last = pe.matmul(ps[w][0:ROWS, 0, 0:D], avT[w][:, c, 0:ROWS], weights[:, c, :],
                                         start=(c == 0), stop=(c == 1))
                    last.then_inc(o_mm[a][w], 1)

                return transposes, attend, turn, project

            def stay_warm(count, bank):
                for i in range(count):
                    pe.matmul(ps[0][:, bank, 0:P], ident[:, 0:P], ident[:, 0:P], start=True, stop=True)

            def run_back(n, a, weights, between, fill=False, warm=(0, 0)):
                lane0, lane1 = (back(n, w, a, weights) for w in lanes)

                def embed(w, part=range(KC)):
                    if fill:
                        front_embed(xT, xT_loaded, 16 * n + 32, FRONT, (w,), part)

                embed(0, range(KC // 2, KC))
                stay_warm(warm[0], FRONT)
                lane0[0]()
                embed(1, range(KC // 2))
                stay_warm(warm[1], FRONT)
                if a == 1:
                    between(LANES)
                if a == 0:
                    lane0[1]()
                    lane1[0]()
                    embed(1, range(KC // 2, KC))
                    lane0[2]()
                    lane1[1]()
                    lane0[3]()
                    lane1[2]()
                    between(0)
                    between(1)
                else:
                    lane1[0]()
                    lane0[1]()
                    lane1[1]()
                    lane0[2]()
                    between(0)
                    lane1[2]()
                    lane0[3]()
                lane1[3]()
                if a == 1:
                    between(1)

            def front_embed(src, loaded, count, bank, of=range(LANES), part=range(KC)):
                for w in of:
                    pe.wait_ge(loaded[w], count)
                    for c in part:
                        last = pe.matmul(ps[w][:, bank, 0:D], src[w][:, c, :], wtok_c[:, c, :],
                                         start=(c == 0), stop=(c == KC - 1))
                    if c == KC - 1:
                        last.then_inc(tok_mm[w], 1)

            def front_queries(m, of=range(LANES)):
                for w in of:
                    pe.wait_ge(qn_ready[w], m + 1)
                    for c in range(2):
                        last = pe.transpose(ps[w][0:WIDE, FRONT, c * P:c * P + ROWS],
                                            qn[w][0:ROWS, :, :].rearrange("p g d -> p (g d)")[:, c * P:c * P + WIDE],
                                            ident[0:ROWS, 0:ROWS])
                    last.then_inc(qnT_mm[w], 1)

            def all_read(read, count):
                for w in lanes:
                    pe.wait_ge(read[w], count)

            def front_scores(m, g, of=range(LANES)):
                for w in of:
                    if g == 0:
                        pe.wait_ge(qnT_ready[w], m + 1)
                    else:
                        pe.wait_ge(raw_ready[w], 4 * m + g)
                    pe.matmul(ps[w][0:ROWS, FRONT, 0:3 * REL], qnT[w][:, g // 2, 0:ROWS],
                              wrel[:, g // 2, (g % 2) * 3 * REL:(g % 2 + 1) * 3 * REL],
                              start=True, stop=True).then_inc(pos_mm[w], 1)

            def fc1(n, j, v, c, small):
                if j == 0:
                    for w in lanes:
                        pe.wait_ge(n2T_ready[w], n + 1)
                        pe.wait_ge(n2T_ready_dve[w], n + 1)
                if j >= GROUPS:
                    pe.wait_ge(gelu_ready, chunk_count(n, j - GROUPS, small))
                if small:
                    parts = {2: ((0, 0, KEEP[2]),), 1: ((0, KEEP[2], KEEP[1]),), 0: ((1, 0, DC),)}[v]
                else:
                    parts = ((0, 0, DC), (1, 0, DC))
                for i in range(CHUNK):
                    w, bank = MLP_BANKS[j % GROUPS]
                    dst = ps[w][:, bank, i * BOTH:(i + 1) * BOTH]
                    cols = slice((c + i) * P, (c + i + 1) * P)
                    for kc, a, b in parts:
                        last = pe.matmul(dst, w1[a:b, kc, cols], blocks(n2T_all[a:b, kc, :]),
                                         start=(kc == 0 and a == 0 and not (small and i > 0)),
                                         stop=(kc == 1 or small), skip_group_check=small)
                last.then_inc(fc1_mm, 1)

            def fc2(n, w, j, v, c, small):
                pe.wait_ge(gelu_ready, chunk_count(n, j, small))
                weights = w2_kept[v] if small else w2
                for i in range(CHUNK):
                    first = j == 0 and i == 0
                    final = j == len(chunks(small)) - 1 and i == CHUNK - 1
                    last = pe.matmul(ps[w][0:ROWS, 0, 0:KEEP[v]], hid[w][:, j, i, 0:ROWS], weights[:, c + i, :],
                                     start=first, stop=final, skip_group_check=True)
                if final:
                    last.then_inc(fc2_mm[w], 1)

            def step(n, small, ahead):
                warm = dict(zip(WARM_PLACES, WARM[0 if not small else 1 if ahead else 2]))

                def queries_between(w):
                    if ahead:
                        if not small:
                            pe.wait_ge(emb_ready[w], n + 3)
                        front_queries(n + 1, (w,))

                def scores_between(w):
                    if ahead and w < LANES:
                        front_scores(n + 1, 3, (w,))
                    elif ahead:
                        front_scores(n + 1, 2)

                for m in range(PAIRS):
                    bank = Q_BANKS[m // 2]
                    if m % 2 == 0 and bank == 0:
                        pe.wait_ge(res_ready[0], n + 1)
                    last = pe.matmul(ps[0][:, bank, (m % 2) * BOTH:(m % 2 + 1) * BOTH], wqk[:, m, :],
                                     blocks(qnT_all[:, m // 3, :]), start=True, stop=True)
                    if m % 2 == 1:
                        last.then_inc(q_mm, 1)
                for w in (1, 0):
                    if w == 0:
                        all_read(raw_ready, 4 * n + 4)
                        stay_warm(warm["values"], FRONT)
                        pe.wait_ge(qw_ready, 3 * n + 3)
                    else:
                        pe.wait_ge(res_ready[1], n + 1)
                    for b in range(2):
                        for r in range(2):
                            for c in range(2):
                                last = pe.matmul(ps[w][r * ROW:r * ROW + TOK, 0, b * DC + c * 48:b * DC + (c + 1) * 48],
                                                 qnT[w][:, c, b * ROW:b * ROW + TOK], every_other(wv[:, c, :], r),
                                                 start=True, stop=True)
                    last.then_inc(v_mm[0][w], 1)
                for w in lanes:
                    for m in range(PAIRS):
                        for b in range(2):
                            cols = slice(b * ROW, b * ROW + TOK)
                            for r in range(2):
                                half = slice(r * ROW, r * ROW + FEAT + 1)
                                last = pe.matmul(ps[w][b * ROW:b * ROW + TOK, 1 + r, m * TOK:(m + 1) * TOK],
                                                 qw[w][half, m, cols], qnT[w][half, m // 3, cols],
                                                 start=True, stop=True)
                    last.then_inc(score_mm[0][w], 1)
                    if w == 0:
                        stay_warm(warm["content_scores"], FRONT)
                        if not small:
                            front_embed(xT, xT_loaded, 16 * n + 32, FRONT, (0,), range(KC // 2))
                run_back(n, 0, wo, queries_between, fill=not small,
                         warm=(warm["first_probs0"], warm["first_probs1"]))
                if ahead:
                    front_scores(n + 1, 0)
                    front_scores(n + 1, 1)
                stay_warm(warm["first_projection"], 2)

                def turn_norm(w):
                    pe.wait_ge(nr_ready[w], n + 1)
                    features(nr, w)(1).then_inc(nT_mm[w], 1)

                turn_norm(0)
                stay_warm(warm["norm_turned"], 2)
                for w in lanes:
                    pe.wait_ge(nT_ready[w], n + 1)
                    for bank, first, done in ((2, 0, q2_mm), (1, D, k2_mm)):
                        for c in range(2):
                            for kc in range(2):
                                cols = wqkv[:, kc, first + c * DC:first + (c + 1) * DC]
                                last = pe.matmul(ps[w][0:DC, bank, c * 2 * TOK:(c + 1) * 2 * TOK], cols,
                                                 tokens(nT, w, kc), start=(kc == 0), stop=(kc == 1))
                        last.then_inc(done[w], 1)
                    if w == 0:
                        turn_norm(1)
                    for b in range(2):
                        for r in range(2):
                            for c in range(2):
                                last = pe.matmul(ps[w][r * ROW:r * ROW + TOK, 0, b * DC:(b + 1) * DC],
                                                 nT[w][:, c, b * ROW:b * ROW + TOK],
                                                 every_other(wqkv[:, c, 2 * D:3 * D], r),
                                                 start=(c == 0), stop=(c == 1))
                    last.then_inc(v_mm[1][w], 1)
                for w in lanes:
                    pe.wait_ge(q2_ready[w], n + 1)
                    pe.wait_ge(k2_ready[w], n + 1)
                    pe.wait_ge(v_ready[1][w], n + 1)
                    for c in range(2):
                        for b in range(2):
                            for g in range(3):
                                part = slice(g * 32, (g + 1) * 32)
                                last = pe.matmul(ps[w][b * ROW:b * ROW + TOK, g, c * 2 * TOK:(c + 1) * 2 * TOK],
                                                 q2[w][part, c, b * ROW:b * ROW + TOK],
                                                 k2[w][part, c, b, :, :].rearrange("p r t -> p (r t)"),
                                                 start=True, stop=True)
                    last.then_inc(score_mm[1][w], 1)
                if ahead:
                    all_read(raw_ready, 4 * n + 6)
                run_back(n, 1, wproj[small], scores_between,
                         warm=(warm["second_probs0"], warm["second_probs1"]))
                stay_warm(warm["second_projection"], 2)
                for w in lanes:
                    pe.wait_ge(nr2_ready[w], n + 1)
                    chunk_each(nr2, w).then_inc(n2T_mm[w], 1)
                todo = chunks(small)
                for j in range(len(todo) + 2):
                    if j < len(todo):
                        fc1(n, j, *todo[j], small)
                    if j >= 2:
                        for w in lanes:
                            fc2(n, w, j - 2, *todo[j - 2], small)

            pe.wait_ge(zeroed_a, 1)
            pe.wait_ge(tok_loaded, TOK_LOADED)
            pe.wait_ge(setup_v, 1)
            for bank, lhs in ((0, gain_768th), (1, c6("ln1_b"))):
                for c in range(KC):
                    last = pe.matmul(ps[0][:, bank, 0:D], lhs[:, c:c + 1].to_broadcast([P, P]), wtok[:, c, :],
                                     start=(c == 0), stop=(c == KC - 1))
                last.then_inc(setup_mm, 1)
            pe.wait_ge(zeroed_a, 2)
            pe.wait_ge(keys_loaded, KEYS_LOADED)
            for m in range(PAIRS):
                for c in range(2):
                    last = pe.matmul(ps[1][:, m // 3, (m % 3) * REL:(m % 3 + 1) * REL], rk[:, c, m * P:(m + 1) * P],
                                     post[:, c, :], start=(c == 0), stop=(c == 1))
            last.then_inc(rel_mm, 1)
            pe.wait_ge(setup_v, 2)
            front_embed(xT_first, first_loaded, 16, FRONT)
            pe.wait_ge(rel_loaded, REL_LOADED)
            pe.wait_ge(rel_ready, 1)
            pe.wait_ge(bias_read, 1)
            for m in range(PAIRS):
                for r in range(2):
                    half = slice(r * DH, (r + 1) * DH)
                    last = pe.matmul(ps[r][0:WIDE, m // 3, (m % 3) * REL:(m % 3 + 1) * REL], wqt[half, m, :],
                                     rel[half, m, :], start=True, stop=True)
            last.then_inc(rel_mm, 1)
            for m in range(PAIRS):
                for r in range(2):
                    half = slice(r * DH, (r + 1) * DH)
                    last = pe.matmul(ps[r][0:WIDE, 2, m * ROW:(m + 1) * ROW], wqc[half, m, :], wkt[half, m, :],
                                     start=True, stop=True)
            last.then_inc(rel_mm, 1)
            pe.wait_ge(rel_ready, 2)
            front_embed(xT, xT_loaded, 16, 1, (0,))
            pe.wait_ge(early_loaded, EARLY)
            pe.wait_ge(zeroed_p, 1)
            all_read(emb_ready, 1)
            front_queries(0)
            front_scores(0, 0)
            front_embed(xT, xT_loaded, 16, 1, (1,))
            for g in range(1, 4):
                front_scores(0, g)
            all_read(emb_ready, 2)
            pe.wait_ge(rel_ready, 3)
            pe.wait_ge(ffn_loaded, FFN_LOADED)
            with pe.Fori(0, LARGE_STEPS) as n:
                step(n, False, True)
            pe.wait_ge(setup_p, 1)
            step(LARGE_STEPS, True, True)
            step(LARGE_STEPS + 1, True, False)


def _chunked(w, rows):
    return w.reshape(-1, rows, w.shape[-1]).transpose(1, 0, 2)


def kernel(**inputs):
    import numpy as np
    import concourse.bacc as bacc
    from concourse.bass_utils import run_bass_kernel_spmd as run

    g = {k: np.asarray(v) for k, v in inputs.items()}
    side = g["x"].shape[-1] // 16
    patches = g["x"].reshape(IMAGES, 3, side, 16, side, 16).transpose(0, 2, 4, 3, 5, 1)
    patches = patches.reshape(STEPS, LANES, 2, TOK, KC, P)
    patches_t = np.zeros((STEPS, LANES, P, KC, 2, ROW), np.float32)
    patches_t[..., 0:TOK] = patches.transpose(0, 1, 5, 4, 2, 3)
    order = [6 * (m // 3) + 3 * r + m % 3 for m in range(PAIRS) for r in range(2)]

    def by_head(weights, bias):
        w = np.zeros((HEADS, DH, ROW), np.float32)
        for n, head in enumerate(order):
            w[n, :, 0:FEAT] = weights[head // 3][:, head % 3 * DH:(head % 3 + 1) * DH].T
            w[n, :, FEAT] = bias[head]
        return w

    def query_side(bias):
        w = np.zeros((PAIRS, 2, DH, 2, ROW), np.float32)
        for n, head in enumerate(by_head(g["L0_attn_Wq"], bias)):
            w[n // 2, n % 2, :, n % 2] = head
        return w.reshape(PAIRS, P, 2 * ROW)[:, :, 0:WIDE].transpose(1, 0, 2)

    w_kt = by_head(g["L0_attn_Wk"], g["L0_attn_bk"].reshape(HEADS, DH))
    w_v = np.zeros((2, ROW, 2, HEADS // 2, DV), np.float32)
    for n, head in enumerate(order):
        cols = slice(head % 3 * DV, (head % 3 + 1) * DV)
        w_v[n % 2, 0:FEAT, n // 6, n % 6] = g["L0_attn_Wv"][head // 3][:, cols]
        w_v[n % 2, FEAT, n // 6, n % 6] = g["L0_attn_bv"].reshape(HEADS, DV)[head]
    w_o = g["L0_attn_Wo"].reshape(HEADS, DV, D)[order].reshape(D, D)
    parity = np.zeros((P, 2), np.float32)
    for r in range(2):
        parity.reshape(P // 32, 2, DV, 2)[:, r, :, r] = 1.0
    columns = {"ln1_g": g["L0_tok_ln1_g"], "ln1_b": g["L0_tok_ln1_b"], "b_fc1": g["L0_ffn_b_fc1"]}
    vectors = {"tok_b": "L0_tok_b", "ln2_g": "L0_tok_ln2_g", "ln2_b": "L0_tok_ln2_b",
               "bo": "L0_attn_bo", "gamma": "L0_attn_gamma", "beta": "L0_attn_beta",
               "b_proj": "L0_ffn_b_proj", "b_fc2": "L0_ffn_b_fc2"}
    positions = g["L0_attn_position_embeds"][1:REL + 1].T
    w_qkv = g["L0_ffn_w_qkv"].reshape(D, 3, PAIRS // 2, 2, 2 * DV)
    w_qkv = np.concatenate([w_qkv[:, 0:2].transpose(0, 1, 3, 2, 4).reshape(D, 2 * D), w_qkv[:, 2].reshape(D, D)],
                           axis=1)
    arrays = {
        "x": patches.reshape(STEPS, LANES, 2, TOK, PATCH),
        "x_t": patches_t.reshape(STEPS, LANES, P, KC, P),
        "w_qc": query_side(g["L0_attn_r_w_bias"]),
        "w_qt": query_side(g["L0_attn_r_r_bias"]),
        "w_tok": _chunked(g["L0_tok_W"].T, P),
        "w_kt": w_kt.reshape(PAIRS, P, ROW).transpose(1, 0, 2),
        "w_v": w_v.reshape(2 * ROW, 2, DC)[0:WIDE],
        "r_kernel": _chunked(g["L0_attn_r_kernel"][:, order].reshape(D, PATCH), DC),
        "pos_t": _chunked(positions, DC),
        "w_o": _chunked(w_o, DC),
        "w_qkv": _chunked(w_qkv, DC),
        "w_proj": _chunked(g["L0_ffn_w_proj"], DC),
        "w_fc1": _chunked(g["L0_ffn_w_fc1"], DC),
        "w_fc2": _chunked(g["L0_ffn_w_fc2"], P),
        "rows": np.stack([g[vectors[k]] for k in ROW_NAMES]),
        "cols6": np.stack([columns[k].reshape(6, P).T for k in COL6_NAMES], axis=1),
        "cols2": np.stack([g["L0_ffn_" + k].reshape(2, DC).T for k in COL2_NAMES], axis=1),
        "gumbel": g["L0_ffn_gumbel_weights"],
        "ident_in": np.concatenate([np.eye(P, dtype=np.float32), parity], axis=1),
    }
    nc = bacc.Bacc("TRN2", target_bir_lowering=False, num_devices=1)
    feeds, args = {}, {}
    for name, a in arrays.items():
        a = np.ascontiguousarray(a)
        feeds[f"{name}_dram"] = a
        args[name] = nc.dram_tensor(f"{name}_dram", a.shape, mybir.dt.from_np(a.dtype), kind="ExternalInput").ap()
    args["out"] = nc.dram_tensor("out_dram", (STEPS, LANES, 2, TOK, D), F32, kind="ExternalOutput").ap()
    vit_tower(nc, **args)
    r = run(nc, [feeds], core_ids=[0])
    return r.results[0]["out_dram"].reshape(IMAGES, TOK, D)
```
